# Optimizing a Trainium2 kernel written in Bass

```python
import numpy as np
import jax
import jax.numpy as jnp

def _softmax(x, axis=-1):
    return jax.nn.softmax(x, axis=axis)

def _gelu(x):
    return jax.nn.gelu(x, approximate=True)

def _silu(x):
    return jax.nn.silu(x)

def _sigmoid(x):
    return jax.nn.sigmoid(x)

def _layernorm(x, axis=-1, eps=1e-05):
    m = jnp.mean(x, axis=axis, keepdims=True)
    v = jnp.var(x, axis=axis, keepdims=True)
    return (x - m) / jnp.sqrt(v + eps)

def _scatter_add(tgt, idx, src, axis=0):
    return tgt.at[idx].add(src)

def _segment_sum(src, seg, n):
    return jax.ops.segment_sum(src, seg, n)
kernel_name = 'mk_xattn_ffn_d1_seqx_r8_5e5af0'

def setup_inputs(seed: int=0):
    np.random.seed(seed)
    _w = jnp.asarray

    def _rec_inputs():
        import jax
        import jax.numpy as jnp
        _rk = jax.random.key(seed)
        x = 7.22e-05 + 1 * jax.random.normal(jax.random.fold_in(_rk, 1), (1, 1024, 128), jnp.float32)
        _lenS = 1024 - jax.random.randint(jax.random.fold_in(_rk, 7), (1,), 0, max(1, 1024 // 4) + 1, jnp.int32)
        _lenS2 = 6404 - jax.random.randint(jax.random.fold_in(_rk, 8), (1,), 0, max(1, 6404 // 4) + 1, jnp.int32)
        _ctx_768P = jax.random.normal(jax.random.fold_in(_rk, 11), (1, 16, 96), jnp.float32)
        _ctx_768c = jax.random.dirichlet(jax.random.fold_in(_rk, 511), 0.3 * jnp.ones((16,), jnp.float32), (1, 6404))
        _ctx_768t = jnp.einsum('bsk,bkd->bsd', _ctx_768c, _ctx_768P)
        _ctx_768t = _ctx_768t * jax.lax.rsqrt(jnp.mean(jnp.square(_ctx_768t)) + 1e-12) * 0.953939
        ctx_768 = -0.000191848 + 0.999787 * (_ctx_768t + 0.3 * jax.random.normal(jax.random.fold_in(_rk, 611), (1, 6404, 96), jnp.float32))
        return (x, ctx_768)
    x, ctx_768 = _rec_inputs()

    def _L0_xattn_setup():
        import jax, jax.numpy as jnp
        import numpy as np
        NUM_HEADS = 16
        CLAMP = 10000.0
        key = jax.random.key(seed)
        ks = jax.random.split(key, 8)
        B, Nq, Nkv, Cq, Ckv = (4, 256, 256, 128, 96)
        s_q = 1.0 / np.sqrt(Cq)
        s_kv = 1.0 / np.sqrt(Ckv)
        return {'query': jax.random.normal(ks[0], (B, Nq, Cq), jnp.float32), 'key_value': jax.random.normal(ks[1], (B, Nkv, Ckv), jnp.float32), 'Wq': jax.random.normal(ks[2], (Cq, Cq), jnp.float32) * s_q, 'bq': jnp.zeros((Cq,), jnp.float32), 'Wk': jax.random.normal(ks[3], (Ckv, Cq), jnp.float32) * s_kv, 'bk': jnp.zeros((Cq,), jnp.float32), 'Wv': jax.random.normal(ks[4], (Ckv, Cq), jnp.float32) * s_kv, 'bv': jnp.zeros((Cq,), jnp.float32), 'Wo': jax.random.normal(ks[5], (Cq, Cq), jnp.float32) * s_q, 'bo': jnp.zeros((Cq,), jnp.float32)}
    _L0_xattn_all = _L0_xattn_setup()
    _L0_xattn_in = {k: v for k, v in _L0_xattn_all.items() if k in ('Wq', 'bq', 'Wk', 'bk', 'Wv', 'bv', 'Wo', 'bo')}
    del _L0_xattn_all

    def _L0_ffn_setup():
        import jax, jax.numpy as jnp
        import numpy as np
        from jax import lax
        B, N, D, H, E, K = (16, 128, 128, 512, 8, 2)
        key = jax.random.key(seed)
        ks = jax.random.split(key, 12)
        s = 0.02
        return {'x': jax.random.normal(ks[0], (B, N, D), jnp.float32), 'alpha': jnp.asarray(0.9, jnp.float32), 'w_gate': jax.random.normal(ks[1], (D, E), jnp.float32) * s, 'b_gate': jnp.zeros((E,), jnp.float32), 'W1m': jax.random.normal(ks[2], (D, H), jnp.float32) * s, 'b1m': jnp.zeros((H,), jnp.float32), 'W2m': jax.random.normal(ks[3], (H, D), jnp.float32) * s, 'b2m': jnp.zeros((D,), jnp.float32), 'W1e': jax.random.normal(ks[4], (E, D, H), jnp.float32) * s, 'b1e': jnp.zeros((E, H), jnp.float32), 'W2e': jax.random.normal(ks[5], (E, H, D), jnp.float32) * s, 'b2e': jnp.zeros((E, D), jnp.float32)}
    _L0_ffn_all = _L0_ffn_setup()
    _L0_ffn_in = {k: v for k, v in _L0_ffn_all.items() if k in ('alpha', 'w_gate', 'b_gate', 'W1m', 'b1m', 'W2m', 'b2m', 'W1e', 'b1e', 'W2e', 'b2e')}
    del _L0_ffn_all
    return {'x': x, 'ctx_768': ctx_768, 'L0_xattn_Wq': _L0_xattn_in['Wq'], 'L0_xattn_bq': _L0_xattn_in['bq'], 'L0_xattn_Wk': _L0_xattn_in['Wk'], 'L0_xattn_bk': _L0_xattn_in['bk'], 'L0_xattn_Wv': _L0_xattn_in['Wv'], 'L0_xattn_bv': _L0_xattn_in['bv'], 'L0_xattn_Wo': _L0_xattn_in['Wo'], 'L0_xattn_bo': _L0_xattn_in['bo'], 'L0_ffn_alpha': _L0_ffn_in['alpha'], 'L0_ffn_w_gate': _L0_ffn_in['w_gate'], 'L0_ffn_b_gate': _L0_ffn_in['b_gate'], 'L0_ffn_W1m': _L0_ffn_in['W1m'], 'L0_ffn_b1m': _L0_ffn_in['b1m'], 'L0_ffn_W2m': _L0_ffn_in['W2m'], 'L0_ffn_b2m': _L0_ffn_in['b2m'], 'L0_ffn_W1e': _L0_ffn_in['W1e'], 'L0_ffn_b1e': _L0_ffn_in['b1e'], 'L0_ffn_W2e': _L0_ffn_in['W2e'], 'L0_ffn_b2e': _L0_ffn_in['b2e']}

def reference(x, ctx_768, L0_xattn_Wq, L0_xattn_bq, L0_xattn_Wk, L0_xattn_bk, L0_xattn_Wv, L0_xattn_bv, L0_xattn_Wo, L0_xattn_bo, L0_ffn_alpha, L0_ffn_w_gate, L0_ffn_b_gate, L0_ffn_W1m, L0_ffn_b1m, L0_ffn_W2m, L0_ffn_b2m, L0_ffn_W1e, L0_ffn_b1e, L0_ffn_W2e, L0_ffn_b2e):
    import jax
    import jax.numpy as jnp

    def _L0_xattn_ref(query, key_value, Wq, bq, Wk, bk, Wv, bv, Wo, bo):
        import jax, jax.numpy as jnp
        import numpy as np
        NUM_HEADS = 16
        CLAMP = 10000.0
        B, Nq, Cq = query.shape
        Nkv = key_value.shape[1]
        H = NUM_HEADS
        D = Cq // H
        scale = D ** (-0.5)
        q = (query @ Wq + bq).reshape(B, Nq, H, D).transpose(0, 2, 1, 3)
        k = (key_value @ Wk + bk).reshape(B, Nkv, H, D).transpose(0, 2, 1, 3)
        v = (key_value @ Wv + bv).reshape(B, Nkv, H, D).transpose(0, 2, 1, 3)
        attn = jnp.einsum('bhqd,bhkd->bhqk', q, k) * scale
        attn = jnp.clip(attn, -CLAMP, CLAMP)
        attn = jax.nn.softmax(attn, axis=-1)
        attn = jnp.where(jnp.any(jnp.isnan(attn)), jnp.asarray(1.0 / Nkv, attn.dtype), attn)
        x = jnp.einsum('bhqk,bhkd->bqhd', attn, v).reshape(B, Nq, Cq)
        return x @ Wo + bo

    def _L0_ffn_ref(x, alpha, w_gate, b_gate, W1m, b1m, W2m, b2m, W1e, b1e, W2e, b2e):
        import jax, jax.numpy as jnp
        import numpy as np
        from jax import lax
        B, N, D, H, E, K = (16, 128, 128, 512, 8, 2)
        main = jax.nn.gelu(x @ W1m + b1m) @ W2m + b2m
        logits = jnp.mean(x, axis=1) @ w_gate + b_gate
        probs = jax.nn.softmax(logits, axis=-1)
        top_vals, top_idx = lax.top_k(probs, K)
        gate_w = top_vals / jnp.sum(top_vals, axis=-1, keepdims=True)
        W1g = W1e[top_idx]
        b1g = b1e[top_idx]
        W2g = W2e[top_idx]
        b2g = b2e[top_idx]
        h = jax.nn.gelu(jnp.einsum('bnd,bkdh->bknh', x, W1g) + b1g[:, :, None, :])
        eo = jnp.einsum('bknh,bkhd->bknd', h, W2g) + b2g[:, :, None, :]
        expert_out = jnp.einsum('bk,bknd->bnd', gate_w, eo)
        a = jnp.clip(alpha, 0.1, 1.0)
        return a * main + (1.0 - a) * expert_out
    x = x + _L0_xattn_ref(_layernorm(x, axis=-1), ctx_768, L0_xattn_Wq, L0_xattn_bq, L0_xattn_Wk, L0_xattn_bk, L0_xattn_Wv, L0_xattn_bv, L0_xattn_Wo, L0_xattn_bo)
    x = x + _L0_ffn_ref(_layernorm(x, axis=-1), L0_ffn_alpha, L0_ffn_w_gate, L0_ffn_b_gate, L0_ffn_W1m, L0_ffn_b1m, L0_ffn_W2m, L0_ffn_b2m, L0_ffn_W1e, L0_ffn_b1e, L0_ffn_W2e, L0_ffn_b2e)
    return x

_drawn_inputs = setup_inputs


def setup_inputs(seed=0):
    import zlib

    import numpy as np

    out = dict(_drawn_inputs(seed))
    spreads = {'L0_xattn_bq': (0.0, 0.495),
     'L0_xattn_bk': (0.0, 2.0),
     'L0_xattn_bv': (0.0, 0.1),
     'L0_xattn_bo': (0.0, 0.1),
     'L0_ffn_b_gate': (0.0, 2.0),
     'L0_ffn_b1m': (0.0, 0.47),
     'L0_ffn_b2m': (0.0, 0.1),
     'L0_ffn_b1e': (0.0, 0.8),
     'L0_ffn_b2e': (0.0, 0.8)}
    factors = {'L0_ffn_w_gate': 8.0, 'L0_ffn_W1e': 8.0, 'L0_ffn_W2e': 8.0}
    for name, (base, spread) in spreads.items():
        noise = np.random.default_rng([zlib.crc32(name.encode()), seed]).standard_normal(out[name].shape)
        drawn = base * np.exp(spread * noise) if base else spread * noise
        out[name] = jnp.asarray(drawn.astype(out[name].dtype))
    for name, factor in factors.items():
        out[name] = (out[name] * factor).astype(out[name].dtype)
    return out
```

```python
from contextlib import ExitStack

import concourse.bass as bass
from concourse import mybir

F32, BF16, I32, U32 = mybir.dt.float32, mybir.dt.bfloat16, mybir.dt.int32, mybir.dt.uint32
ALU, ACT, AX = mybir.AluOpType, mybir.ActivationFunctionType, mybir.AxisListType

P = 128
NQ, C, CK, NK = 1024, 128, 96, 6404
H, D = 16, 8
E, HID, TOPK = 8, 512, 2
SCALE = float(D) ** -0.5
CLAMP, EPS = 10000.0, 1e-5
SAFE_RANGE = 60.0
SAFE_SCORE = 0.999 * CLAMP

QT = NQ // P
FULL = NK // P
TAIL = NK - FULL * P
BANK = 512
KCH = -(-NK // BANK)
NHALF = NQ // BANK
GH = 4
NG = H // GH
QUAD = P // GH
TERMS = [(0, 0), (0, 1), (1, 0), (0, 2), (2, 0), (1, 1), (1, 2), (2, 1)]
ROWS = len(TERMS) * D
NSEG = 5
SEG_T = FULL // NSEG
SEG_C = SEG_T * P
SP_T = 5
SP_C = SP_T * P
NSP = FULL // SP_T
CPT = 3
CH_G = FULL * NHALF * GH + NHALF
TL_G = CH_G // CPT
QD_G = FULL * NHALF + NHALF
VCH = -(-(FULL + 1) // 4)
FFN_LOADS = 9
NPR = 3
CB = HID // P
assert CH_G % CPT == 0 and FULL % NSEG == 0 and FULL % SP_T == 0


def chunk(c):
    if c >= FULL * NHALF * GH:
        return FULL, c - FULL * NHALF * GH, None
    return c // (NHALF * GH), c % (NHALF * GH) // GH, c % GH


def step_of(c):
    kt, half, _ = chunk(c)
    return kt * NHALF + half


def seg_cols(s):
    return s * SEG_C, (s + 1) * SEG_C if s < NSEG - 1 else NK


def split_cols(s):
    return s * SP_C, (s + 1) * SP_C if s < NSP - 1 else NK


def build(nc, x, ctx, wq, bq, wk, bk, wv, bv, wo, bo, alpha, w_gate, b_gate, w1m, b1m, w2m, b2m,
          w1e, b1e, w2e, b2e, out):
    kst_dram = nc.dram_tensor("kst_dram", (H, ROWS, NK), BF16, kind="Internal").ap()
    qst_dram = nc.dram_tensor("qst_dram", (H, ROWS, NQ), BF16, kind="Internal").ap()

    with ExitStack() as stack:
        def sb(name, shape, dt=F32):
            return stack.enter_context(nc.sbuf_tensor(name, shape, dt))

        def sem(name):
            return stack.enter_context(nc.semaphore(name))

        ident = sb("ident", [P, P])
        ones = sb("ones", [P, P])
        hmask = sb("hmask", [P, H])
        xres = sb("xres", [P, QT, C])
        xn = sb("xn", [P, QT, C])
        xnT = sb("xnT", [C, NQ])
        qT = sb("qT", [C, NQ])
        bob = sb("bob", [P, C])
        bqc = sb("bqc", [C, 1])
        wq_sb = sb("wq_sb", [C, C])
        wk_sb = sb("wk_sb", [CK + 1, C])
        wv_sb = sb("wv_sb", [CK + 1, C])
        wog = sb("wog", [P, NG, C])
        stats = sb("stats", [P, QT, 6])
        mv = sb("mv", [P, QT, 2])
        rstd = sb("rstd", [P, 4, QT])
        region_ctx = sb("region_ctx", [P, FULL * CK])
        ctx_sb = region_ctx[:, :].rearrange("p (t c) -> p t c", t=FULL)
        w1s = region_ctx[:, 0:TOPK * HID].rearrange("p (e n) -> p e n", e=TOPK)
        w2s = region_ctx[:, TOPK * HID:2 * TOPK * HID].rearrange("p (e c n) -> p e c n", e=TOPK, c=CB)
        ctx_tail = sb("ctx_tail", [TAIL, CK])
        region_ctxT = sb("region_ctxT", [P, NK])
        ctxT = region_ctxT[0:CK + 1, :]
        tailT = sb("tailT", [CK + 1, P])
        region_kT = sb("region_kT", [P, NK])
        kT = region_kT
        att = region_kT[:, 0:NG * NQ].rearrange("p (g n) -> p g n", g=NG)
        oraw = region_kT[:, NG * NQ:NG * NQ + NQ]
        oden = region_kT[:, NG * NQ + NQ:NG * NQ + 2 * NQ]
        kparts = sb("kparts", [P, 2, 3, SP_C + TAIL], BF16)
        krest = sb("krest", [P, 2, SP_C + TAIL])
        region_k = sb("region_k", [P, 2 * (FULL * P + QUAD)], BF16)
        kst = region_k[:, :].rearrange("p (w n) -> p w n", w=2)
        srow = region_k[:, 0:2 * NK].bitcast(F32)
        vall = sb("vall", [P, FULL + 1, C])
        region_v = sb("region_v", [P, FULL * P])
        vst = region_v[:, :].rearrange("p (t n) -> p t n", t=FULL)
        neq = region_v[:, 0:NK // 2].bitcast(BF16)
        q_abs = region_v[:, 0:NQ]
        q_rest = region_v[:, NQ:2 * NQ]
        qparts = region_v[:, 2 * NQ:2 * NQ + 3 * NQ // 2].bitcast(BF16).rearrange("p (a n) -> p a n", a=3)
        vtail = sb("vtail", [P, P])
        qst = sb("qst", [P, H // 2, NQ], BF16)
        hid = [region_ctxT[:, 0:CB * NQ].rearrange("p (c n) -> p c n", c=CB),
               region_v[:, 0:CB * NQ].rearrange("p (c n) -> p c n", c=CB)]
        ksum = sb("ksum", [P, KCH + NHALF])
        kmax = sb("kmax", [P, KCH])
        kmin = sb("kmin", [P, KCH])
        kst4 = sb("kst4", [P, 8])
        bounds = sb("bounds", [P, 2 * H])
        gcol = sb("gcol", [2 * H, NHALF + 1])
        grow = sb("grow", [1, 4])
        flag = sb("flag", [1, 1], I32)
        w1m_sb = sb("w1m_sb", [C, HID])
        w2m_sb = sb("w2m_sb", [P, CB, C])
        b1rows = sb("b1rows", [(E + 1) * CB, P])
        b1T = sb("b1T", [P, (E + 1) * CB])
        b1s = sb("b1s", [P, TOPK, CB])
        b2rows = sb("b2rows", [1, 3, C])
        wg = sb("wg", [C, E])
        bg = sb("bg", [1, E])
        msum = sb("msum", [C, 4])
        gate = sb("gate", [1, 12, E])
        topi = sb("topi", [1, 8], U32)
        mix = sb("mix", [1, 4])
        mixb = sb("mixb", [P, 3])
        bsum = sb("bsum", [1, 3, C])
        qm = sb("qm", [C, P])
        pT = sb("pT", [P, 2, P])
        gen = sb("gen", [P, 8])
        attq = region_v[:, NK // 2:NK // 2 + QT * C].rearrange("p (t n) -> p t n", t=QT)
        attqT = region_v[:, NK // 2 + QT * C:NK // 2 + QT * C + NQ]
        vmean = sb("vmean", [P, 2, C])

        probs = region_ctx[:, 0:NPR * CPT * BANK].rearrange("p (b n) -> p b n", b=NPR)

        ps = [stack.enter_context(nc.psum_tensor(f"ps{i}", [P, CPT * BANK], F32)) for i in range(2)]
        po = [stack.enter_context(nc.psum_tensor(f"po{i}", [P, BANK], F32)) for i in range(NHALF)]

        x_in, wts_in, bo_in, wo_in, tail_in, ffn_in = (sem(n) for n in ("x_in", "wts_in", "bo_in", "wo_in", "tail_in", "ffn_in"))
        ctx_in = [sem(f"ctx_in{i}") for i in range(NSEG)]
        const_zero, const_ready, pads_ready = sem("const_zero"), sem("const_ready"), sem("pads_ready")
        dve_step, fast_step, gen_step, gen_loop_step, tail_step = (sem(n) for n in ("dve_step", "fast_step", "gen_step", "gen_loop_step", "tail_step"))
        var_ready, std_ready, xn_ready = sem("var_ready"), sem("std_ready"), sem("xn_ready")
        xnT_psum, xnT_ready, q_psum, q_ready = sem("xnT_psum"), sem("xnT_ready"), sem("q_psum"), sem("q_ready")
        ctxT_psum, ctxT_ready, tailT_ready = sem("ctxT_psum"), sem("ctxT_ready"), sem("tailT_ready")
        k_psum, k_ready, v_psum, v_done = sem("k_psum"), sem("k_ready"), sem("v_psum"), sem("v_done")
        centre_ready, k1_ready, krest_ready, k2_ready, k3_ready = (sem(n) for n in ("centre_ready", "k1_ready", "krest_ready", "k2_ready", "k3_ready"))
        kparts_stored = [sem("kparts_stored0"), sem("kparts_stored1")]
        qparts_ready, qparts_stored, qst_in = sem("qparts_ready"), sem("qparts_stored"), sem("qst_in")
        bounds_ready, bound_psum, gcol_ready, grow_psum, flag_ready = (sem(n) for n in ("bounds_ready", "bound_psum", "gcol_ready", "grow_psum", "flag_ready"))
        kst_in = [sem(f"kst_in{s}") for s in range(NSEG)]
        vst_ready = sem("vst_ready")
        scores_ready, exp_ready, pv_done, o_taken = sem("scores_ready"), sem("exp_ready"), sem("pv_done"), sem("o_taken")
        den_moved, att_ready, rows_psum = sem("den_moved"), sem("att_ready"), sem("rows_psum")
        attention_done = sem("attention_done")
        gq_ready, gs_psum, gs_copied, gs_shifted, gexp_ready, gpT_psum, gpT_ready, go_done, gfin_psum, gfin_ready, g_moved = (
            sem(n) for n in ("gq_ready", "gs_psum", "gs_copied", "gs_shifted", "gexp_ready", "gpT_psum", "gpT_ready", "go_done", "gfin_psum", "gfin_ready", "g_moved"))
        y_psum, logit_psum, exp_gate, topk_ready, mix_ready, mixb_psum = (
            sem(n) for n in ("y_psum", "logit_psum", "exp_gate", "topk_ready", "mix_ready", "mixb_psum"))
        experts_in, w2_scaled, hid_psum, hid_ready, ffn2_done, bsum_ready, b1s_ready, rows_taken = (
            sem(n) for n in ("experts_in", "w2_scaled", "hid_psum", "hid_ready", "ffn2_done", "bsum_ready", "b1s_ready", "rows_taken"))
        msum_ready, ffn_psum, res_ready, out_stored = sem("msum_ready"), sem("ffn_psum"), sem("res_ready"), sem("out_stored")

        block = stack.enter_context(nc.Block())

        def move_sums(sp, g):
            sp.wait_ge(o_taken, NHALF * (g + 1))
            if g >= 1:
                sp.wait_ge(att_ready, g)
            for j in range(GH):
                sp.dma_start(oden[QUAD * j:QUAD * j + D, :], oraw[QUAD * j + D:QUAD * j + 2 * D, :]).then_inc(den_moved, 16)

        def evac_k(act, c):
            a, b = c * BANK, min((c + 1) * BANK, NK)
            act.wait_ge(k_psum, c + 1)
            act.activation(kT[:, a:b], ps[1][:, (c % CPT) * BANK:(c % CPT) * BANK + b - a], ACT.Copy,
                           accum_out=ksum[:, c:c + 1]).then_inc(k_ready, 1)

        def second_part(act, s):
            a, b = split_cols(s)
            act.wait_ge(krest_ready, s + 1)
            act.activation(kparts[:, s % 2, 1, 0:b - a], krest[:, s % 2, 0:b - a], ACT.Copy).then_inc(k2_ready, 1)

        @block.sync
        def _(sp):
            sp.dma_start(xres[:, :, :], x[0].rearrange("(t p) c -> p t c", p=P)).then_inc(x_in, 16)
            for dst, src in ((wk_sb[0:CK, :], wk), (wk_sb[CK:CK + 1, :], bk), (wq_sb[:, :], wq), (bqc[:, :], bq)):
                sp.dma_start(dst, src).then_inc(wts_in, 16)
            rows = ctx[0, 0:FULL * P, :].rearrange("(p t) c -> p t c", t=FULL)
            for i in range(NSEG):
                sp.dma_start(ctx_sb[:, i * SEG_T:(i + 1) * SEG_T, :], rows[:, i * SEG_T:(i + 1) * SEG_T, :]).then_inc(ctx_in[i], 16)
            sp.dma_start(ctx_tail[:, :], ctx[0, FULL * P:NK, :]).then_inc(tail_in, 16)
            sp.wait_ge(const_ready, 4)
            for j in range(GH):
                sp.dma_start(wog[QUAD * j:QUAD * j + D, :, :],
                             wo.rearrange("(g j d) n -> j d g n", g=NG, j=GH)[j]).then_inc(wo_in, 16)
            sp.wait_ge(qparts_ready, 3)
            for t, (_, b) in enumerate(TERMS):
                sp.dma_start(qst_dram[:, t * D:(t + 1) * D, :], qparts[:, b, :]).then_inc(qparts_stored, 16)
            sp.wait_ge(qparts_stored, 16 * len(TERMS))
            sp.dma_start(qst[:, :, :], qst_dram.rearrange("(w j) r n -> (j r) w n", j=2)).then_inc(qst_in, 16)
            for s in range(NSP):
                a, b = split_cols(s)
                sp.wait_ge(k1_ready, s + 1)
                sp.wait_ge(k2_ready, s + 1)
                sp.wait_ge(k3_ready, s + 1)
                for t, (part, _) in enumerate(TERMS):
                    sp.dma_start(kst_dram[:, t * D:(t + 1) * D, a:b],
                                 kparts[:, s % 2, part, 0:b - a]).then_inc(kparts_stored[s % 2], 16)
            sp.wait_ge(flag_ready, 1)
            safe = sp.value_load(flag[0:1, 0:1], min_val=0, max_val=1)
            with sp.If(safe != 0):
                for g in range(NG):
                    for s in range(NSEG):
                        a, b = seg_cols(s)
                        if g == 0:
                            last = min((s + 1) * SEG_T // SP_T, NSP) - 1
                            sp.wait_ge(kparts_stored[last % 2], 16 * len(TERMS) * (last // 2 + 1))
                            sp.wait_ge(kparts_stored[(last - 1) % 2], 16 * len(TERMS) * ((last - 1) // 2 + 1))
                        else:
                            chunks = (s + 1) * SEG_T * NHALF * GH if s < NSEG - 1 else CH_G
                            sp.wait_ge(scores_ready, (g - 1) * TL_G + (chunks - 1) // CPT + 1)
                        sp.dma_start(kst[:, :, a:b],
                                     kst_dram[GH * g:GH * (g + 1), :, a:b].rearrange("(w j) r n -> (j r) w n", j=2)
                                     ).then_inc(kst_in[s], 16)
                    if g >= 1:
                        move_sums(sp, g - 1)
                move_sums(sp, NG - 1)
            with sp.Else():
                for n in (0, 1):
                    sp.wait_ge(kparts_stored[n], 16 * len(TERMS) * (NSP // 2))
                sp.wait_ge(gfin_ready, 3)
                for h in range(H):
                    j = h % GH
                    sp.dma_start(att[QUAD * j:QUAD * j + D, h // GH, :],
                                 attqT[h * D:(h + 1) * D, :]).then_inc(g_moved, 16)
            sp.wait_ge(topk_ready, 1)
            for e in range(TOPK):
                i = sp.value_load(topi[0:1, e:e + 1], min_val=0, max_val=E - 1)
                sp.dma_start(w1s[:, e, :], w1e[bass.ds(i, 1), :, :].rearrange("e d n -> (e d) n")).then_inc(experts_in, 16)
                sp.dma_start(w2s[:, e, :, :], w2e[bass.ds(i, 1), :, :].rearrange("e (c p) d -> p (e c) d", p=P)).then_inc(experts_in, 16)
                sp.dma_start(b2rows[0:1, 1 + e, :], b2e[bass.ds(i, 1), :]).then_inc(experts_in, 16)
            for n in range(NHALF):
                sp.wait_ge(res_ready, n + 1)
                sp.dma_start(out[0, n * BANK:(n + 1) * BANK, :].rearrange("(t p) c -> p t c", p=P),
                             xn[:, n * QT // 2:(n + 1) * QT // 2, :]).then_inc(out_stored, 16)
            sp.wait_ge(out_stored, 16 * NHALF)

        @block.gpsimd
        def _(pool):
            pool.memset(ident[:, :], 0.0).then_inc(const_zero, 1)
            pool.memset(ones[:, :], 1.0).then_inc(const_ready, 1)
            pool.memset(hmask[:, :], 1.0).then_inc(const_zero, 1)
            pool.wait_ge(const_zero, 1)
            pool.affine_select(out=ident[:, :], in_=ident[:, :], compare_op=ALU.not_equal, fill=1.0, base=0,
                               pattern=[[-1, P]], channel_multiplier=1).then_inc(const_ready, 1)
            pool.wait_ge(const_zero, 2)
            pool.affine_select(out=hmask[:, :], in_=hmask[:, :], compare_op=ALU.is_ge, fill=0.0, base=0,
                               pattern=[[-D, H]], channel_multiplier=1).then_inc(const_zero, 1)
            pool.wait_ge(const_zero, 3)
            pool.affine_select(out=hmask[:, :], in_=hmask[:, :], compare_op=ALU.is_ge, fill=0.0, base=D - 1,
                               pattern=[[D, H]], channel_multiplier=-1).then_inc(const_ready, 1)
            pool.memset(wog[:, :, :], 0.0).then_inc(const_ready, 1)
            pool.wait_ge(const_ready, 4)
            pool.memset(region_ctxT[CK:CK + 1, :], 1.0).then_inc(pads_ready, 1)
            pool.wait_ge(pads_ready, 1)
            pool.memset(tailT[:, :], 0.0).then_inc(pads_ready, 1)
            pool.wait_ge(pads_ready, 2)
            pool.memset(kst[:, :, NK:], 0.0).then_inc(pads_ready, 1)
            for dst, src in ((wv_sb[0:CK, :], wv), (wv_sb[CK:CK + 1, :], bv)):
                pool.dma_start(dst, src).then_inc(bo_in, 16)
            for dst, src in ((bsum[0:1, 0, :], bo), (mix[0:1, 3:4], alpha), (wg[:, :], w_gate), (bg[:, :], b_gate),
                             (w1m_sb[:, :], w1m), (w2m_sb[:, :, :], w2m.rearrange("(c p) d -> p c d", p=P)),
                             (b1rows[0:E * CB, :], b1e.rearrange("e (c p) -> (e c) p", p=P)),
                             (b1rows[E * CB:(E + 1) * CB, :], b1m.rearrange("a (c p) -> (a c) p", p=P)),
                             (b2rows[0:1, 0, :], b2m)):
                pool.dma_start(dst, src).then_inc(ffn_in, 16)

        @block.scalar
        def _(act):
            act.wait_ge(var_ready, 1)
            act.activation(rstd[:, 1, :], rstd[:, 0, :], ACT.Sqrt).then_inc(std_ready, 1)
            for n in range(NHALF):
                act.wait_ge(xnT_psum, n + 1)
                act.activation(xnT[:, n * BANK:(n + 1) * BANK], po[n][:, :], ACT.Copy).then_inc(xnT_ready, 1)
            act.wait_ge(wts_in, 64)
            for n in range(NHALF):
                act.wait_ge(q_psum, n + 1)
                act.activation(qT[:, n * BANK:(n + 1) * BANK], po[n][:, :], ACT.Identity, bias=bqc[:, 0:1],
                               accum_out=ksum[:, KCH + n:KCH + n + 1]).then_inc(q_ready, 1)
            for c in range(KCH):
                a, b = c * BANK, min((c + 1) * BANK, NK)
                act.wait_ge(ctxT_psum, c + 1)
                act.activation(ctxT[0:CK, a:b], ps[0][0:CK, (c % CPT) * BANK:(c % CPT) * BANK + b - a], ACT.Copy).then_inc(ctxT_ready, 1)
                if c >= 1:
                    evac_k(act, c - 1)
            evac_k(act, KCH - 1)
            act.wait_ge(centre_ready, 1)
            for s in range(NSP):
                a, b = split_cols(s)
                if s >= 2:
                    act.wait_ge(kparts_stored[s % 2], 16 * len(TERMS) * (s // 2))
                act.activation(kparts[:, s % 2, 0, 0:b - a], kT[:, a:b], ACT.Identity, bias=kst4[:, 3:4]).then_inc(k1_ready, 1)
                if s >= 1:
                    second_part(act, s - 1)
            second_part(act, NSP - 1)
            act.wait_ge(flag_ready, 1)
            safe = act.value_load(flag[0:1, 0:1], min_val=0, max_val=1)
            with act.If(safe != 0):
                for t in range(NG * TL_G):
                    act.wait_ge(scores_ready, t + 1)
                    if t >= NPR:
                        g, i = divmod(t - NPR, TL_G)
                        act.wait_ge(pv_done, g * QD_G + step_of(CPT * i + CPT - 1) + 1)
                    act.activation(probs[:, t % NPR, :], ps[t % 2][:, :], ACT.Exp, scale=SCALE).then_inc(exp_ready, 1)
            with act.Else():
                with act.Fori(0, H) as h:
                    with act.Fori(0, QT) as t:
                        act.wait_ge(gs_shifted, h * QT + t + 1)
                        act.activation(srow[:, :], srow[:, :], ACT.Exp, bias=gen[:, 1:2],
                                       accum_out=gen[:, 2:3]).then_inc(gexp_ready, 1)
            act.wait_ge(var_ready, 2)
            act.activation(rstd[:, 1, :], rstd[:, 0, :], ACT.Sqrt).then_inc(std_ready, 1)
            for n in range(NHALF):
                act.wait_ge(xnT_psum, NHALF + n + 1)
                act.activation(xnT[:, n * BANK:(n + 1) * BANK], ps[1][:, n * BANK:(n + 1) * BANK], ACT.Copy,
                               accum_out=msum[:, n:n + 1]).then_inc(xnT_ready, 1)
            act.wait_ge(msum_ready, 2)
            act.activation(gate[0:1, 2, :], gate[0:1, 1, :], ACT.Exp, accum_out=gate[0:1, 3, 0:1]).then_inc(exp_gate, 1)
            for n in range((1 + TOPK) * CB * NHALF):
                e, r = divmod(n, CB * NHALF)
                cb, half = divmod(r, NHALF)
                act.wait_ge(hid_psum, n + 1)
                if e == 1 and r == 0:
                    act.wait_ge(b1s_ready, 1)
                if e == 2 and r == 0:
                    act.wait_ge(ffn2_done, 1)
                bias = b1T[:, E * CB + cb:E * CB + cb + 1] if e == 0 else b1s[:, e - 1, cb:cb + 1]
                bank = n % 6
                act.activation(hid[e % 2][:, cb, half * BANK:(half + 1) * BANK],
                               ps[bank // CPT][:, (bank % CPT) * BANK:(bank % CPT + 1) * BANK],
                               ACT.Gelu_apprx_tanh, bias=bias).then_inc(hid_ready, 1)

        @block.vector
        def _(dve):
            v = nc.vector

            def chain(step):
                count = [0]

                def link(ins):
                    count[0] += 1
                    ins.then_inc(step, 1)
                    dve.wait_ge(step, count[0])
                return link

            link = chain(dve_step)

            def layernorm(nth, link):
                for t in range(QT):
                    last = v.bn_stats(stats[:, t, :], xres[:, t, :])
                link(last)
                for t in range(QT):
                    last = v.bn_aggr(mv[:, t, :], stats[:, t, :])
                link(last)
                v.tensor_scalar(rstd[:, 0, :], mv[:, :, 1], EPS, None, ALU.add).then_inc(var_ready, 1)
                dve.wait_ge(std_ready, nth)
                link(v.reciprocal(rstd[:, 2, :], rstd[:, 1, :]))
                link(v.tensor_tensor(rstd[:, 3, :], rstd[:, 0, :], rstd[:, 2, :], ALU.mult))
                link(v.tensor_tensor(rstd[:, 2, :], rstd[:, 3, :], rstd[:, 1, :], ALU.add))
                link(v.tensor_scalar(rstd[:, 3, :], rstd[:, 2, :], 0.5, None, ALU.mult))
                link(v.reciprocal(rstd[:, 2, :], rstd[:, 3, :]))
                for t in range(QT):
                    v.tensor_scalar(xn[:, t, :], xres[:, t, :], mv[:, t, 0:1], rstd[:, 2, t:t + 1],
                                    ALU.subtract, ALU.mult).then_inc(xn_ready, 1)

            dve.wait_ge(x_in, 16)
            layernorm(1, link)
            dve.wait_ge(q_ready, NHALF)
            v.tensor_copy(qparts[:, 0, :], qT[:, :]).then_inc(qparts_ready, 1)
            dve.wait_ge(qparts_ready, 1)
            link(v.tensor_tensor(q_rest[:, :], qT[:, :], qparts[:, 0, :], ALU.subtract))
            v.tensor_copy(qparts[:, 1, :], q_rest[:, :]).then_inc(qparts_ready, 1)
            dve.wait_ge(qparts_ready, 2)
            v.tensor_tensor(qparts[:, 2, :], q_rest[:, :], qparts[:, 1, :], ALU.subtract).then_inc(qparts_ready, 1)
            link(v.memset(vtail[:, :], 0.0))
            link(v.tensor_scalar(q_abs[:, :], qT[:, :], -1.0, None, ALU.mult))
            link(v.tensor_tensor(q_abs[:, :], q_abs[:, :], qT[:, :], ALU.max))
            for c in range(KCH):
                a, b = c * BANK, min((c + 1) * BANK, NK)
                if c == KCH - 1:
                    dve.wait_ge(ctxT_ready, KCH)
                    dve.wait_ge(pads_ready, 2)
                    for j in range(GH):
                        last = v.tensor_copy(tailT[:, QUAD * j:QUAD * j + TAIL], ctxT[:, FULL * P:NK])
                    last.then_inc(tailT_ready, 1)
                dve.wait_ge(k_ready, c + 1)
                v.tensor_reduce(kmax[:, c:c + 1], kT[:, a:b], AX.X, ALU.max)
                last = v.tensor_reduce(kmin[:, c:c + 1], kT[:, a:b], AX.X, ALU.min)
            link(last)
            link(v.tensor_reduce(kst4[:, 0:1], kmax[:, :], AX.X, ALU.max))
            link(v.tensor_reduce(kst4[:, 1:2], kmin[:, :], AX.X, ALU.min))
            link(v.tensor_tensor(kst4[:, 2:3], kst4[:, 0:1], kst4[:, 1:2], ALU.add))
            link(v.tensor_scalar(kst4[:, 2:3], kst4[:, 2:3], 0.5, None, ALU.mult))
            v.tensor_scalar(kst4[:, 3:4], kst4[:, 2:3], -1.0, None, ALU.mult).then_inc(centre_ready, 1)
            link(v.tensor_tensor(kst4[:, 4:5], kst4[:, 0:1], kst4[:, 1:2], ALU.subtract))
            link(v.tensor_scalar(kst4[:, 5:6], kst4[:, 1:2], -1.0, None, ALU.mult))
            link(v.tensor_tensor(kst4[:, 5:6], kst4[:, 5:6], kst4[:, 0:1], ALU.max))
            dve.wait_ge(const_ready, 4)
            link(v.tensor_scalar(bounds[:, 0:H], hmask[:, :], kst4[:, 4:5], 0.5 * SCALE / SAFE_RANGE, ALU.mult, ALU.mult))
            v.tensor_scalar(bounds[:, H:2 * H], hmask[:, :], kst4[:, 5:6], SCALE / SAFE_SCORE, ALU.mult, ALU.mult).then_inc(bounds_ready, 1)
            link(v.tensor_reduce(kst4[:, 6:7], ksum[:, :], AX.X, ALU.add))
            v.tensor_scalar(kst4[:, 7:8], kst4[:, 6:7], 0.0, None, ALU.mult).then_inc(bounds_ready, 1)

            def first_rest(s):
                a, b = split_cols(s)
                dve.wait_ge(k1_ready, s + 1)
                if s >= 2:
                    dve.wait_ge(k2_ready, s - 1)
                v.scalar_tensor_tensor(krest[:, s % 2, 0:b - a], kT[:, a:b], kst4[:, 2:3], kparts[:, s % 2, 0, 0:b - a],
                                       ALU.subtract, ALU.subtract).then_inc(krest_ready, 1)

            def third_part(s):
                a, b = split_cols(s)
                dve.wait_ge(k2_ready, s + 1)
                v.tensor_tensor(kparts[:, s % 2, 2, 0:b - a], krest[:, s % 2, 0:b - a], kparts[:, s % 2, 1, 0:b - a],
                                ALU.subtract).then_inc(k3_ready, 1)

            first_rest(0)
            dve.wait_ge(bound_psum, 1)
            link(v.tensor_reduce(gcol[:, 0:1], ps[0][0:2 * H, 0:NQ], AX.X, ALU.max))
            v.tensor_copy(gcol[:, 1:2], gcol[:, 0:1]).then_inc(gcol_ready, 1)
            third_part(0)
            dve.wait_ge(grow_psum, 1)
            link(v.tensor_reduce(grow[:, 0:1], ps[0][0:1, 0:2 * H], AX.X, ALU.max))
            link(v.tensor_tensor(grow[:, 1:2], grow[:, 0:1], ps[0][0:1, BANK:BANK + 1], ALU.add))
            v.tensor_scalar(flag[:, :], grow[:, 1:2], 1.0, None, ALU.is_lt).then_inc(flag_ready, 1)
            for s in range(1, NSP):
                first_rest(s)
                third_part(s)
            for c in range(VCH):
                n = min(4, FULL + 1 - 4 * c)
                dve.wait_ge(v_psum, c + 1)
                v.tensor_copy(vall[:, 4 * c:4 * c + n, :],
                              po[c % 2][:, 0:n * P].rearrange("p (t n) -> p t n", t=n)).then_inc(v_done, 1)
            dve.wait_ge(rows_psum, 1)
            link(v.tensor_copy(bob[:, :], po[0][:, 0:C]))
            for t in range(QT):
                last = v.tensor_tensor(xres[:, t, :], xres[:, t, :], bob[:, :], ALU.add)
            link(last)
            link(v.tensor_copy(b1T[:, :], po[1][:, 0:(E + 1) * CB]))
            link(v.tensor_scalar(mix[:, 0:1], mix[:, 3:4], 0.1, 1.0, ALU.max, ALU.min))
            v.tensor_scalar(gate[0:1, 7, 0:1], mix[:, 0:1], -1.0, 1.0, ALU.mult, ALU.add).then_inc(rows_taken, 1)
            dve.wait_ge(rows_taken, 1)

            dve.wait_ge(qparts_stored, 16 * len(TERMS))
            dve.wait_ge(bound_psum, 1)
            safe = dve.value_load(flag[0:1, 0:1], min_val=0, max_val=1)
            with dve.If(safe != 0):
                flink = chain(fast_step)
                dve.wait_ge(pads_ready, 3)
                flink(v.memset(region_v[:, :], 0.0))
                for j in range(GH):
                    v.memset(vst[:, :, QUAD * j + D:QUAD * j + 2 * D], 1.0)
                    last = v.memset(vtail[QUAD * j:QUAD * j + TAIL, QUAD * j + D:QUAD * j + 2 * D], 1.0)
                flink(last)

                def refill(g, s):
                    t0, t1 = s * SEG_T, (s + 1) * SEG_T
                    if g >= 1:
                        dve.wait_ge(pv_done, (g - 1) * QD_G + (t1 * NHALF if s < NSEG - 1 else QD_G))
                    for j in range(GH if s == NSEG - 1 else 0):
                        r = slice(QUAD * j, QUAD * (j + 1))
                        ch = (g * GH + j) * D
                        v.tensor_copy(vtail[r, QUAD * j:QUAD * j + D], vall[r, FULL, ch:ch + D])
                    v.tensor_copy(vst[:, t0:t1, :].rearrange("p t (j m) -> p t j m", j=GH)[:, :, :, 0:D],
                                  vall[:, t0:t1, g * GH * D:(g + 1) * GH * D].rearrange("p t (j d) -> p t j d", j=GH)
                                  ).then_inc(vst_ready, 1)

                dve.wait_ge(v_done, VCH)
                for s in range(NSEG):
                    refill(0, s)
                flink(v.memset(oden[:, :], 1.0))
                for g in range(NG):
                    for s in range(NSEG - 1):
                        if g + 1 < NG:
                            refill(g + 1, s)
                    for n in range(NHALF):
                        dve.wait_ge(pv_done, g * QD_G + FULL * NHALF + n + 1)
                        if g >= 1 and n == 0:
                            dve.wait_ge(att_ready, g)
                        v.tensor_copy(oraw[:, n * BANK:(n + 1) * BANK], po[n][:, :]).then_inc(o_taken, 1)
                    if g + 1 < NG:
                        refill(g + 1, NSEG - 1)
                    dve.wait_ge(den_moved, 16 * GH * (g + 1))
                    flink(v.reciprocal(att[:, g, :], oden[:, :]))
                    v.tensor_tensor(att[:, g, :], att[:, g, :], oraw[:, :], ALU.mult
                                    ).then_inc(att_ready if g < NG - 1 else attention_done, 1)
            with dve.Else():
                glink = chain(gen_step)
                glink(v.memset(gen[:, :], 0.0))
                dve.wait_ge(v_done, VCH)
                dve.wait_ge(pads_ready, 3)
                with dve.Fori(0, H) as h:
                    with dve.Fori(0, QT) as t:
                        nth = h * QT + t
                        v.tensor_scalar(qm[:, :], qT[:, bass.ds(t * P, P)], hmask[:, bass.ds(h, 1)], None, ALU.mult).then_inc(gq_ready, 1)
                        for c in range(KCH):
                            a, b = c * BANK, min((c + 1) * BANK, NK)
                            dve.wait_ge(gs_psum, nth * KCH + c + 1)
                            v.tensor_copy(srow[:, a:b], ps[1][:, (c % 2) * BANK:(c % 2) * BANK + b - a]).then_inc(gs_copied, 1)
                        dve.wait_ge(gs_copied, (nth + 1) * KCH)

                        def lstep(ins, n):
                            ins.then_inc(gen_loop_step, 1)
                            dve.wait_ge(gen_loop_step, nth * 8 + n)

                        lstep(v.tensor_tensor(neq[:, :], srow[:, :], srow[:, :], ALU.not_equal), 1)
                        lstep(v.tensor_reduce(gen[:, 3:4], neq[:, :], AX.X, ALU.max), 2)
                        lstep(v.tensor_tensor(gen[:, 0:1], gen[:, 0:1], gen[:, 3:4], ALU.max), 3)
                        lstep(v.tensor_scalar(srow[:, :], srow[:, :], SCALE, CLAMP, ALU.mult, ALU.min), 4)
                        lstep(v.tensor_scalar(srow[:, :], srow[:, :], -CLAMP, None, ALU.max), 5)
                        lstep(v.tensor_reduce(gen[:, 4:5], srow[:, :], AX.X, ALU.max), 6)
                        v.tensor_scalar(gen[:, 1:2], gen[:, 4:5], -1.0, None, ALU.mult).then_inc(gs_shifted, 1)
                        for kt in range(FULL + 1):
                            rows = P if kt < FULL else TAIL
                            dve.wait_ge(gpT_psum, nth * (FULL + 1) + kt + 1)
                            if kt >= 2:
                                dve.wait_ge(go_done, nth * (FULL + 1) + kt - 1)
                            v.tensor_copy(pT[0:rows, kt % 2, :], ps[0][0:rows, (kt % 2) * BANK:(kt % 2) * BANK + P]).then_inc(gpT_ready, 1)
                        dve.wait_ge(go_done, (nth + 1) * (FULL + 1))
                        lstep(v.reciprocal(gen[:, 5:6], gen[:, 2:3]), 7)
                        lstep(v.tensor_scalar(region_v[:, bass.ds(NK // 2 + t * C + h * D, D)], po[0][:, 0:D],
                                              gen[:, 5:6], None, ALU.mult), 8)
                v.tensor_copy(gen[:, 6:7], gen[:, 0:1]).then_inc(gfin_ready, 1)
                dve.wait_ge(gfin_psum, 1)
                glink(v.tensor_scalar(vmean[:, 0, :], po[1][:, 0:C], 1.0 / NK, None, ALU.mult))
                glink(v.tensor_scalar(gen[:, 7:8], po[0][:, 0:1], 0.5, None, ALU.is_gt))
                glink(v.tensor_scalar(vmean[:, 1, :].bitcast(U32), ones[:, :], gen[:, 7:8], None, ALU.mult))
                for t in range(QT):
                    last = v.copy_predicated(attq[:, t, :], vmean[:, 1, :].bitcast(U32), vmean[:, 0, :])
                last.then_inc(gfin_ready, 1)
                dve.wait_ge(gfin_psum, 2)
                glink(v.tensor_copy(attqT[:, :], ps[0][:, 0:NQ]))
                v.memset(region_kT[:, 0:NG * NQ], 0.0).then_inc(gfin_ready, 1)
                dve.wait_ge(g_moved, 16 * H)
                v.memset(gen[:, 7:8], 0.0).then_inc(attention_done, 1)

            tlink = chain(tail_step)
            for n in range(NHALF):
                dve.wait_ge(y_psum, n + 1)
                last = v.tensor_tensor(xres[:, n * QT // 2:(n + 1) * QT // 2, :],
                                       ps[0][:, n * BANK:(n + 1) * BANK].rearrange("p (t c) -> p t c", c=C),
                                       xres[:, n * QT // 2:(n + 1) * QT // 2, :], ALU.add)
            tlink(last)
            layernorm(2, tlink)
            dve.wait_ge(xnT_ready, 2 * NHALF)
            v.tensor_tensor(msum[:, 2:3], msum[:, 0:1], msum[:, 1:2], ALU.add).then_inc(msum_ready, 1)
            dve.wait_ge(logit_psum, 1)
            dve.wait_ge(ffn_in, 16 * FFN_LOADS)
            tlink(v.scalar_tensor_tensor(gate[0:1, 0, :], po[0][0:1, 0:E], 1.0 / NQ, bg[:, :], ALU.mult, ALU.add))
            tlink(v.tensor_reduce(gate[0:1, 4, 0:1], gate[0:1, 0, :], AX.X, ALU.max))
            v.tensor_scalar(gate[0:1, 1, :], gate[0:1, 0, :], gate[0:1, 4, 0:1], None, ALU.subtract).then_inc(msum_ready, 1)
            dve.wait_ge(exp_gate, 1)
            tlink(v.reciprocal(gate[0:1, 4, 1:2], gate[0:1, 3, 0:1]))
            tlink(v.tensor_scalar(gate[0:1, 5, :], gate[0:1, 2, :], gate[0:1, 4, 1:2], None, ALU.mult))
            tlink(v.max(gate[0:1, 6, :], gate[0:1, 5, :]))
            v.max_index(topi[:, :], gate[0:1, 6, :], gate[0:1, 5, :]).then_inc(topk_ready, 1)
            tlink(v.tensor_tensor(gate[0:1, 4, 2:3], gate[0:1, 6, 0:1], gate[0:1, 6, 1:2], ALU.add))
            tlink(v.reciprocal(gate[0:1, 4, 3:4], gate[0:1, 4, 2:3]))
            v.tensor_scalar(mix[0:1, 1:3], gate[0:1, 6, 0:TOPK], gate[0:1, 4, 3:4], gate[0:1, 7, 0:1], ALU.mult, ALU.mult).then_inc(mix_ready, 1)
            dve.wait_ge(topk_ready, 1)
            for e in range(TOPK):
                i = dve.value_load(topi[0:1, e:e + 1], min_val=0, max_val=E - 1)
                last = v.tensor_copy(b1s[:, e, :], b1T[:, bass.ds(i * CB, CB)])
            last.then_inc(b1s_ready, 1)
            dve.wait_ge(mixb_psum, 1)
            tlink(v.tensor_copy(mixb[:, :], po[1][:, 0:3]))
            v.tensor_scalar(w2m_sb[:, :, :], w2m_sb[:, :, :], mixb[:, 0:1], None, ALU.mult).then_inc(w2_scaled, 1)
            dve.wait_ge(experts_in, 16 * 3 * TOPK)
            for e in range(TOPK):
                v.tensor_scalar(w2s[:, e, :, :], w2s[:, e, :, :], mixb[:, 1 + e:2 + e], None, ALU.mult).then_inc(w2_scaled, 1)
            dve.wait_ge(mix_ready, 1)
            tlink(v.tensor_scalar(bsum[0:1, 1, :], b2rows[0:1, 0, :], mix[0:1, 0:1], None, ALU.mult))
            tlink(v.scalar_tensor_tensor(bsum[0:1, 2, :], b2rows[0:1, 1, :], mix[0:1, 1:2], bsum[0:1, 1, :], ALU.mult, ALU.add))
            v.scalar_tensor_tensor(bsum[0:1, 0, :], b2rows[0:1, 2, :], mix[0:1, 2:3], bsum[0:1, 2, :], ALU.mult, ALU.add).then_inc(bsum_ready, 1)
            for n in range(NHALF):
                dve.wait_ge(ffn_psum, n + 1)
                v.tensor_tensor(xn[:, n * QT // 2:(n + 1) * QT // 2, :],
                                po[n][:, :].rearrange("p (t c) -> p t c", c=C),
                                xres[:, n * QT // 2:(n + 1) * QT // 2, :], ALU.add).then_inc(res_ready, 1)

        @block.tensor
        def _(pe):
            mm, tr = nc.tensor.matmul, nc.tensor.transpose
            pe.wait_ge(const_ready, 4)
            for n in range(NHALF):
                for t in range(n * QT // 2, (n + 1) * QT // 2):
                    pe.wait_ge(xn_ready, t + 1)
                    last = tr(po[n][:, (t % 4) * P:(t % 4 + 1) * P], xn[:, t, :], ident[:, :])
                last.then_inc(xnT_psum, 1)
            pe.wait_ge(wts_in, 64)
            for n in range(NHALF):
                pe.wait_ge(xnT_ready, n + 1)
                mm(po[n][:, :], wq_sb[:, :], xnT[:, n * BANK:(n + 1) * BANK], start=True, stop=True).then_inc(q_psum, 1)

            def ctx_transpose(c):
                if c >= CPT:
                    pe.wait_ge(ctxT_ready, c - CPT + 1)
                at = (c % CPT) * BANK
                for t in range(4 * c, min(4 * c + 4, FULL)):
                    pe.wait_ge(ctx_in[t // SEG_T], 16)
                    last = tr(ps[0][0:CK, at:at + P], ctx_sb[:, t, :], ident[:, :])
                    at += P
                if c == KCH - 1:
                    pe.wait_ge(tail_in, 16)
                    last = tr(ps[0][0:CK, at:at + TAIL], ctx_tail[:, :], ident[0:TAIL, 0:TAIL])
                last.then_inc(ctxT_psum, 1)

            pe.wait_ge(pads_ready, 3)
            ctx_transpose(0)
            ctx_transpose(1)
            for c in range(KCH):
                if c + 2 < KCH:
                    ctx_transpose(c + 2)
                a, b = c * BANK, min((c + 1) * BANK, NK)
                pe.wait_ge(ctxT_ready, c + 1)
                if c >= CPT:
                    pe.wait_ge(k_ready, c - CPT + 1)
                mm(ps[1][:, (c % CPT) * BANK:(c % CPT) * BANK + b - a], wk_sb[:, :], ctxT[:, a:b], start=True, stop=True).then_inc(k_psum, 1)
            pe.wait_ge(bounds_ready, 2)
            for n in range(NHALF):
                last = mm(ps[0][0:2 * H, n * BANK:(n + 1) * BANK], bounds[:, :], q_abs[:, n * BANK:(n + 1) * BANK], start=True, stop=True)
            last.then_inc(bound_psum, 1)
            pe.wait_ge(gcol_ready, 1)
            mm(ps[0][0:1, 0:2 * H], gcol[:, 1:2], ident[0:2 * H, 0:2 * H], start=True, stop=True)
            mm(ps[0][0:1, BANK:BANK + 1], kst4[:, 7:8], ones[:, 0:1], start=True, stop=True).then_inc(grow_psum, 1)
            pe.wait_ge(bo_in, 32)
            pe.wait_ge(q_ready, NHALF)
            pe.wait_ge(tailT_ready, 1)
            for c in range(VCH):
                if c >= 2:
                    pe.wait_ge(v_done, c - 1)
                for t in range(4 * c, min(4 * c + 4, FULL + 1)):
                    lhsT = ctxT[:, t * P:(t + 1) * P] if t < FULL else tailT[:, :]
                    last = mm(po[c % 2][:, (t % 4) * P:(t % 4 + 1) * P], lhsT, wv_sb[:, :], start=True, stop=True)
                last.then_inc(v_psum, 1)
            pe.wait_ge(ffn_in, 16 * FFN_LOADS)
            pe.wait_ge(v_done, VCH)
            mm(po[0][:, 0:C], ones[0:1, :], bsum[0:1, 0, :], start=True, stop=True)
            tr(po[1][:, 0:(E + 1) * CB], b1rows[:, :], ident[0:(E + 1) * CB, 0:(E + 1) * CB]).then_inc(rows_psum, 1)
            pe.wait_ge(rows_taken, 1)
            pe.wait_ge(flag_ready, 1)
            safe = pe.value_load(flag[0:1, 0:1], min_val=0, max_val=1)
            with pe.If(safe != 0):
                def score_tile(t):
                    g, i = divmod(t, TL_G)
                    if t >= 2:
                        pe.wait_ge(exp_ready, t - 1)
                    for m in range(CPT):
                        kt, half, j = chunk(CPT * i + m)
                        if (CPT * i + m) % (SEG_T * NHALF * GH) == 0 and kt < FULL:
                            pe.wait_ge(kst_in[kt // SEG_T], 16 * (g + 1))
                        queries = slice(half * BANK, (half + 1) * BANK)
                        dst = ps[t % 2][:, m * BANK:(m + 1) * BANK]
                        for jj in ([j] if kt < FULL else range(GH)):
                            rows, w = slice(ROWS * (jj % 2), ROWS * (jj % 2 + 1)), jj // 2
                            if kt < FULL:
                                last = mm(dst, kst[rows, w, kt * P:(kt + 1) * P], qst[rows, g * GH // 2 + w, queries], start=True, stop=True)
                            else:
                                last = mm(dst[QUAD * jj:QUAD * (jj + 1), :], kst[rows, w, kt * P:kt * P + QUAD],
                                          qst[rows, g * GH // 2 + w, queries], start=True, stop=True, skip_group_check=True)
                    last.then_inc(scores_ready, 1)

                def values_step(g, n):
                    kt, half = divmod(n, NHALF)
                    if half == 0 and kt < FULL and kt % SEG_T == 0:
                        pe.wait_ge(vst_ready, g * NSEG + kt // SEG_T + 1)
                    if g >= 1 and kt == 0:
                        pe.wait_ge(o_taken, (g - 1) * NHALF + half + 1)
                    for j in range(GH if kt < FULL else 1):
                        c = n * GH + j if kt < FULL else FULL * NHALF * GH + half
                        t, m = divmod(c, CPT)
                        src = probs[:, (g * TL_G + t) % NPR, m * BANK:(m + 1) * BANK]
                        if kt < FULL:
                            last = mm(po[half][QUAD * j:QUAD * (j + 1), :], vst[:, kt, QUAD * j:QUAD * (j + 1)], src,
                                      start=(kt == 0), stop=False, skip_group_check=True)
                        else:
                            last = mm(po[half][:, :], vtail[:, :], src, start=False, stop=True, skip_group_check=True)
                    last.then_inc(pv_done, 1)

                pe.wait_ge(qst_in, 16)
                score_tile(0)
                score_tile(1)
                for t in range(NG * TL_G):
                    g, i = divmod(t, TL_G)
                    if t + 2 < NG * TL_G:
                        score_tile(t + 2)
                    else:
                        pe.wait_ge(exp_ready, t + 1)
                    for n in range(QD_G):
                        c = (n + 1) * GH - 1 if n < FULL * NHALF else FULL * NHALF * (GH - 1) + n
                        if c // CPT == i:
                            values_step(g, n)
            with pe.Else():
                with pe.Fori(0, H) as h:
                    with pe.Fori(0, QT) as t:
                        nth = h * QT + t
                        pe.wait_ge(gq_ready, nth + 1)
                        for c in range(KCH):
                            a, b = c * BANK, min((c + 1) * BANK, NK)
                            if c >= 2:
                                pe.wait_ge(gs_copied, nth * KCH + c - 1)
                            mm(ps[1][:, (c % 2) * BANK:(c % 2) * BANK + b - a], qm[:, :], kT[:, a:b], start=True, stop=True).then_inc(gs_psum, 1)
                        pe.wait_ge(gexp_ready, nth + 1)
                        for kt in range(FULL + 1):
                            rows = P if kt < FULL else TAIL
                            if kt >= 2:
                                pe.wait_ge(gpT_ready, nth * (FULL + 1) + kt - 1)
                            tr(ps[0][0:rows, (kt % 2) * BANK:(kt % 2) * BANK + P], srow[:, kt * P:kt * P + rows], ident[:, :]).then_inc(gpT_psum, 1)
                            pe.wait_ge(gpT_ready, nth * (FULL + 1) + kt + 1)
                            mm(po[0][:, 0:D], pT[0:rows, kt % 2, :], vall[0:rows, kt, bass.ds(h * D, D)],
                               start=(kt == 0), stop=(kt == FULL)).then_inc(go_done, 1)
                pe.wait_ge(gfin_ready, 1)
                mm(po[0][:, 0:1], ones[:, :], gen[:, 6:7], start=True, stop=True)
                for kt in range(FULL + 1):
                    rows = P if kt < FULL else TAIL
                    last = mm(po[1][:, 0:C], ones[0:rows, :], vall[0:rows, kt, :], start=(kt == 0), stop=(kt == FULL))
                last.then_inc(gfin_psum, 1)
                pe.wait_ge(gfin_ready, 2)
                for t in range(QT):
                    last = tr(ps[0][:, t * P:(t + 1) * P], attq[:, t, :], ident[:, :])
                last.then_inc(gfin_psum, 1)
            pe.wait_ge(attention_done, 1)
            pe.wait_ge(wo_in, 16 * GH)
            for t in range(QT):
                for g in range(NG):
                    last = mm(ps[0][:, t * P:(t + 1) * P], att[:, g, t * P:(t + 1) * P], wog[:, g, :], start=(g == 0), stop=(g == NG - 1))
                if t % (QT // NHALF) == QT // NHALF - 1:
                    last.then_inc(y_psum, 1)
            for n in range(NHALF):
                for t in range(n * QT // 2, (n + 1) * QT // 2):
                    pe.wait_ge(xn_ready, QT + t + 1)
                    last = tr(ps[1][:, t * P:(t + 1) * P], xn[:, t, :], ident[:, :])
                last.then_inc(xnT_psum, 1)
            pe.wait_ge(msum_ready, 1)
            mm(po[0][0:1, 0:E], msum[:, 2:3], wg[:, :], start=True, stop=True).then_inc(logit_psum, 1)

            def first_layer(e):
                for r in range(CB * NHALF):
                    n = e * CB * NHALF + r
                    cb, half = divmod(r, NHALF)
                    if n >= 6:
                        pe.wait_ge(hid_ready, n - 5)
                    w = w1m_sb[:, cb * P:(cb + 1) * P] if e == 0 else w1s[:, e - 1, cb * P:(cb + 1) * P]
                    bank = n % 6
                    mm(ps[bank // CPT][:, (bank % CPT) * BANK:(bank % CPT + 1) * BANK], w,
                       xnT[:, half * BANK:(half + 1) * BANK], start=True, stop=True).then_inc(hid_psum, 1)

            def second_layer(e):
                pe.wait_ge(hid_ready, (e + 1) * CB * NHALF)
                pe.wait_ge(w2_scaled, e + 1)
                if e == TOPK:
                    pe.wait_ge(bsum_ready, 1)
                w2 = w2m_sb if e == 0 else w2s[:, e - 1, :, :]
                for t in range(QT):
                    dst = po[t // 4][:, (t % 4) * P:(t % 4 + 1) * P]
                    for cb in range(CB):
                        last = mm(dst, hid[e % 2][:, cb, t * P:(t + 1) * P], w2[:, cb, :],
                                  start=(e == 0 and cb == 0 and t % 4 == 0), stop=False, skip_group_check=True)
                    if e == TOPK:
                        last = mm(dst, ones[0:1, :], bsum[0:1, 0, :], start=False, stop=True, skip_group_check=True)
                        if t % 4 == 3:
                            last.then_inc(ffn_psum, 1)
                if e < TOPK:
                    last.then_inc(ffn2_done, 1)

            first_layer(0)
            pe.wait_ge(mix_ready, 1)
            mm(po[1][:, 0:3], ones[0:1, :], mix[0:1, 0:3], start=True, stop=True).then_inc(mixb_psum, 1)
            second_layer(0)
            pe.wait_ge(experts_in, 16 * 3 * TOPK)
            first_layer(1)
            first_layer(2)
            second_layer(1)
            second_layer(2)


_OUT = ((1, NQ, C), "float32")


def kernel(x, ctx_768, L0_xattn_Wq, L0_xattn_bq, L0_xattn_Wk, L0_xattn_bk, L0_xattn_Wv, L0_xattn_bv, L0_xattn_Wo,
           L0_xattn_bo, L0_ffn_alpha, L0_ffn_w_gate, L0_ffn_b_gate, L0_ffn_W1m, L0_ffn_b1m, L0_ffn_W2m, L0_ffn_b2m,
           L0_ffn_W1e, L0_ffn_b1e, L0_ffn_W2e, L0_ffn_b2e):
    import numpy as np
    import concourse.bacc as bacc
    from concourse.bass_utils import run_bass_kernel_spmd

    shaped = {
        "x": x, "ctx": ctx_768, "wq": L0_xattn_Wq, "bq": np.reshape(L0_xattn_bq, (C, 1)), "wk": L0_xattn_Wk,
        "bk": np.reshape(L0_xattn_bk, (1, C)), "wv": L0_xattn_Wv, "bv": np.reshape(L0_xattn_bv, (1, C)),
        "wo": L0_xattn_Wo, "bo": np.reshape(L0_xattn_bo, (1, C)), "alpha": np.reshape(L0_ffn_alpha, (1, 1)),
        "w_gate": L0_ffn_w_gate, "b_gate": np.reshape(L0_ffn_b_gate, (1, E)), "w1m": L0_ffn_W1m,
        "b1m": np.reshape(L0_ffn_b1m, (1, HID)), "w2m": L0_ffn_W2m, "b2m": np.reshape(L0_ffn_b2m, (1, C)),
        "w1e": L0_ffn_W1e, "b1e": L0_ffn_b1e, "w2e": L0_ffn_W2e, "b2e": L0_ffn_b2e,
    }
    nc = bacc.Bacc("TRN2", target_bir_lowering=False, num_devices=1)
    arrays, aps = {}, {}
    for name, value in shaped.items():
        a = np.ascontiguousarray(value)
        arrays[f"in_{name}"] = a
        aps[name] = nc.dram_tensor(f"in_{name}", a.shape, mybir.dt.from_np(a.dtype), kind="ExternalInput").ap()
    shape, dtype = _OUT
    out = nc.dram_tensor("result", shape, mybir.dt.from_np(np.dtype(dtype)), kind="ExternalOutput").ap()
    build(nc, **aps, out=out)
    r = run_bass_kernel_spmd(nc, [arrays], core_ids=[0])
    return r.results[0]["result"]
```

```python
from contextlib import ExitStack

import concourse.bass as bass
from concourse import mybir

F32, BF16, I32, U32 = mybir.dt.float32, mybir.dt.bfloat16, mybir.dt.int32, mybir.dt.uint32
ALU, ACT, AX = mybir.AluOpType, mybir.ActivationFunctionType, mybir.AxisListType

P = 128
NQ, C, CK, NK = 1024, 128, 96, 6404
H, D = 16, 8
E, HID, TOPK = 8, 512, 2
SCALE = float(D) ** -0.5
CLAMP, EPS = 10000.0, 1e-5
SAFE_RANGE = 60.0
SAFE_SCORE = 0.999 * CLAMP

QT = NQ // P
FULL = NK // P
TAIL = NK - FULL * P
BANK = 512
KCH = -(-NK // BANK)
NHALF = NQ // BANK
GH = 4
NG = H // GH
QUAD = P // GH
PARTS = 3
ROWS = PARTS * PARTS * D
SET = PARTS * D
NSEG = 10
SEG_T = FULL // NSEG
SEG_C = SEG_T * P
NSB = 3
CPT = 2
CH_G = FULL * NHALF * GH + NHALF
TL_G = CH_G // CPT
QD_G = FULL * NHALF + NHALF
VCH = -(-(FULL + 1) // 4)
FFN_LOADS = 9
CTX_LOADS = 5
NPR = 4
CB = HID // P
assert CH_G % CPT == 0 and FULL % NSEG == 0


def chunk(c):
    if c >= FULL * NHALF * GH:
        return FULL, c - FULL * NHALF * GH, None
    return c // (NHALF * GH), c % (NHALF * GH) // GH, c % GH


def step_of(c):
    kt, half, _ = chunk(c)
    return kt * NHALF + half


def seg_cols(s):
    return s * SEG_C, (s + 1) * SEG_C if s < NSEG - 1 else NK


def build(nc, x, ctx, wq, bq, wk, bk, wv, bv, wo, bo, alpha, w_gate, b_gate, w1m, b1m, w2m, b2m,
          w1e, b1e, w2e, b2e, out):
    k_dram = nc.dram_tensor("k_dram", (H, PARTS, D, NK), BF16, kind="Internal").ap()
    q_dram = nc.dram_tensor("q_dram", (H, PARTS, D, NQ), BF16, kind="Internal").ap()

    with ExitStack() as stack:
        def sb(name, shape, dt=F32):
            return stack.enter_context(nc.sbuf_tensor(name, shape, dt))

        def sem(name):
            return stack.enter_context(nc.semaphore(name))

        ident = sb("ident", [P, P])
        ones = sb("ones", [P, P])
        hmask = sb("hmask", [P, H])
        xres = sb("xres", [P, QT, C])
        xn = sb("xn", [P, QT, C])
        xnT = sb("xnT", [C, NQ])
        qT = sb("qT", [C, NQ])
        bob = sb("bob", [P, C])
        bqc = sb("bqc", [C, 1])
        bkc = sb("bkc", [C, 1])
        wq_sb = sb("wq_sb", [C, C])
        wk_sb = sb("wk_sb", [CK, C])
        wv_sb = sb("wv_sb", [CK + 1, C])
        wog = sb("wog", [P, NG, C])
        stats = sb("stats", [P, QT, 6])
        mv = sb("mv", [P, QT, 2])
        rstd = sb("rstd", [P, 4, QT])
        region_ctx = sb("region_ctx", [P, FULL * CK])
        ctx_sb = region_ctx[:, :].rearrange("p (t c) -> p t c", t=FULL)
        w1s = region_ctx[:, 0:TOPK * HID].rearrange("p (e n) -> p e n", e=TOPK)
        w2s = region_ctx[:, TOPK * HID:2 * TOPK * HID].rearrange("p (e c n) -> p e c n", e=TOPK, c=CB)
        ctx_tail = sb("ctx_tail", [TAIL, CK])
        region_ctxT = sb("region_ctxT", [P, FULL * P + QUAD])
        ctxT = region_ctxT[0:CK + 1, 0:NK]
        tailT = sb("tailT", [CK + 1, P])
        region_kT = sb("region_kT", [P, NK])
        kT = region_kT
        att = region_kT[:, 0:NG * NQ].rearrange("p (g n) -> p g n", g=NG)
        oraw = region_kT[:, NG * NQ:NG * NQ + NQ]
        oden = region_kT[:, NG * NQ + NQ:NG * NQ + 2 * NQ]
        kparts = sb("kparts", [P, 2, PARTS, SEG_C + TAIL], BF16)
        krest = sb("krest", [P, 2, SEG_C + TAIL])
        region_k = sb("region_k", [P, FULL * P + QUAD])
        kst = [r[:, :].bitcast(BF16).rearrange("p (w n) -> p w n", w=2) for r in (region_k, region_ctxT)]
        srow = region_k[:, 0:NK]
        vall = sb("vall", [P, FULL + 1, C])
        region_v = sb("region_v", [P, FULL * P])
        vst = region_v[:, :].rearrange("p (t n) -> p t n", t=FULL)
        neq = region_v[:, 0:NK // 2].bitcast(BF16)
        q_abs = xn[:, :, :].rearrange("p t c -> p (t c)")
        free_k = (FULL * P + QUAD) // 2
        q_rest = region_k[:, free_k:free_k + NQ]
        qparts = region_k[:, free_k + NQ:free_k + NQ + PARTS * NQ // 2].bitcast(BF16).rearrange("p (a n) -> p a n", a=PARTS)
        vtail = sb("vtail", [P, P])
        qst = sb("qst", [ROWS, 2, GH, NQ], BF16)
        hid = [region_ctxT[:, 0:CB * NQ].rearrange("p (c n) -> p c n", c=CB),
               region_v[:, 0:CB * NQ].rearrange("p (c n) -> p c n", c=CB)]
        ksum = sb("ksum", [P, KCH + NHALF])
        kmax = sb("kmax", [P, KCH])
        kcol = sb("kcol", [P, 8])
        bounds = sb("bounds", [P, 2 * H])
        gcol = sb("gcol", [2 * H, NHALF + 1])
        grow = sb("grow", [1, 4])
        flag = sb("flag", [1, 1], I32)
        w1m_sb = sb("w1m_sb", [C, HID])
        w2m_sb = sb("w2m_sb", [P, CB, C])
        b1rows = sb("b1rows", [(E + 1) * CB, P])
        b1T = sb("b1T", [P, (E + 1) * CB])
        b1s = sb("b1s", [P, TOPK, CB])
        b2rows = sb("b2rows", [1, 3, C])
        wg = sb("wg", [C, E])
        bg = sb("bg", [1, E])
        msum = sb("msum", [C, 4])
        gate = sb("gate", [1, 12, E])
        topi = sb("topi", [1, 8], U32)
        mix = sb("mix", [1, 4])
        mixb = sb("mixb", [P, 3])
        bsum = sb("bsum", [1, 3, C])
        qm = sb("qm", [C, P])
        pT = sb("pT", [P, 2, P])
        gen = sb("gen", [P, 8])
        attq = region_v[:, NK // 2:NK // 2 + QT * C].rearrange("p (t n) -> p t n", t=QT)
        attqT = region_v[:, NK // 2 + QT * C:NK // 2 + QT * C + NQ]
        vmean = sb("vmean", [P, 2, C])

        probs = region_ctx[:, 0:NPR * CPT * BANK].rearrange("p (b n) -> p b n", b=NPR)

        ps = [stack.enter_context(nc.psum_tensor(f"ps{i}", [P, CPT * BANK], F32)) for i in range(NSB)]
        po = [stack.enter_context(nc.psum_tensor(f"po{i}", [P, BANK], F32)) for i in range(NHALF)]

        def bank(i, rows=P, cols=BANK):
            return ps[i // CPT][0:rows, i % CPT * BANK:i % CPT * BANK + cols]

        x_in, wts_in, bo_in, wo_in, tail_in, ffn_in = (sem(n) for n in ("x_in", "wts_in", "bo_in", "wo_in", "tail_in", "ffn_in"))
        ctx_in = [sem(f"ctx_in{i}") for i in range(CTX_LOADS)]
        const_zero, const_ready, pads_ready = sem("const_zero"), sem("const_ready"), sem("pads_ready")
        dve_step, fast_step, gen_step, gen_loop_step, tail_step = (sem(n) for n in ("dve_step", "fast_step", "gen_step", "gen_loop_step", "tail_step"))
        var_ready, std_ready, xn_ready = sem("var_ready"), sem("std_ready"), sem("xn_ready")
        xnT_psum, xnT_ready, q_psum, q_ready = sem("xnT_psum"), sem("xnT_ready"), sem("q_psum"), sem("q_ready")
        ctxT_psum, ctxT_ready, tailT_ready = sem("ctxT_psum"), sem("ctxT_ready"), sem("tailT_ready")
        k_psum, k_ready, v_psum, v_done = sem("k_psum"), sem("k_ready"), sem("v_psum"), sem("v_done")
        kparts_ready = sem("kparts_ready")
        kparts_stored = [sem("kparts_stored0"), sem("kparts_stored1")]
        qparts_ready, qparts_stored = sem("qparts_ready"), sem("qparts_stored")
        qst_in = [sem("qst_in0"), sem("qst_in1")]
        bounds_ready, bound_psum, gcol_ready, grow_psum, flag_ready = (sem(n) for n in ("bounds_ready", "bound_psum", "gcol_ready", "grow_psum", "flag_ready"))
        kst_in = [sem(f"kst_in{s}") for s in range(NSEG)]
        vst_ready = sem("vst_ready")
        scores_ready, exp_ready, pv_done, o_taken = sem("scores_ready"), sem("exp_ready"), sem("pv_done"), sem("o_taken")
        den_moved, att_ready, rows_psum = sem("den_moved"), sem("att_ready"), sem("rows_psum")
        attention_done = sem("attention_done")
        gq_ready, gs_psum, gs_copied, gs_shifted, gexp_ready, gpT_psum, gpT_ready, go_done, gfin_psum, gfin_ready, g_moved = (
            sem(n) for n in ("gq_ready", "gs_psum", "gs_copied", "gs_shifted", "gexp_ready", "gpT_psum", "gpT_ready", "go_done", "gfin_psum", "gfin_ready", "g_moved"))
        y_psum, logit_psum, exp_gate, topk_ready, mix_ready, mixb_psum = (
            sem(n) for n in ("y_psum", "logit_psum", "exp_gate", "topk_ready", "mix_ready", "mixb_psum"))
        experts_in, w2_scaled, hid_psum, hid_ready, ffn2_done, bsum_ready, b1s_ready, rows_taken = (
            sem(n) for n in ("experts_in", "w2_scaled", "hid_psum", "hid_ready", "ffn2_done", "bsum_ready", "b1s_ready", "rows_taken"))
        msum_ready, ffn_psum, res_ready, out_stored = sem("msum_ready"), sem("ffn_psum"), sem("res_ready"), sem("out_stored")

        block = stack.enter_context(nc.Block())

        def store_k(sp, s):
            a, b = seg_cols(s)
            sp.wait_ge(kparts_ready, s + 1)
            for part in range(PARTS):
                sp.dma_start(k_dram[:, part, :, a:b],
                             kparts[:, s % 2, part, 0:b - a]).then_inc(kparts_stored[s % 2], 16)

        def load_k(sp, g, s):
            a, b = seg_cols(s)
            if g == 0:
                sp.wait_ge(kparts_stored[s % 2], 16 * PARTS * (s // 2 + 1))
            for r in range(2):
                rows = k_dram[GH * g + 2 * r:GH * g + 2 * r + 2, :, :, a:b].rearrange("w a d n -> (a d) w n")
                for m in range(PARTS):
                    sp.dma_start(kst[r][SET * m:SET * (m + 1), :, a:b], rows).then_inc(kst_in[s], 16)

        def load_q(sp, g):
            if g >= 2:
                sp.wait_ge(scores_ready, (g - 1) * TL_G)
            for m in range(PARTS):
                rows = q_dram[GH * g:GH * (g + 1), m, :, :].rearrange("w d n -> d w n")
                for a in range(PARTS):
                    sp.dma_start(qst[SET * m + D * a:SET * m + D * (a + 1), g % 2, :, :], rows).then_inc(qst_in[g % 2], 16)

        def move_sums(sp, g):
            sp.wait_ge(o_taken, NHALF * (g + 1))
            if g >= 1:
                sp.wait_ge(att_ready, g)
            for j in range(GH):
                sp.dma_start(oden[QUAD * j:QUAD * j + D, :], oraw[QUAD * j + D:QUAD * j + 2 * D, :]).then_inc(den_moved, 16)

        def evac_k(act, c):
            a, b = c * BANK, min((c + 1) * BANK, NK)
            act.wait_ge(k_psum, c + 1)
            act.activation(kT[:, a:b], bank(3 + c % 3, P, b - a), ACT.Copy,
                           accum_out=ksum[:, c:c + 1]).then_inc(k_ready, 1)

        def evac_v(act, c):
            n = min(4, FULL + 1 - 4 * c)
            act.wait_ge(v_psum, c + 1)
            act.activation(vall[:, 4 * c:4 * c + n, :].rearrange("p t n -> p (t n)"), po[c % 2][:, 0:n * P], ACT.Copy).then_inc(v_done, 1)

        @block.sync
        def _(sp):
            rows = ctx[0, 0:FULL * P, :].rearrange("(p t) c -> p t c", t=FULL)
            sp.dma_start(xres[:, :, :], x[0].rearrange("(t p) c -> p t c", p=P)).then_inc(x_in, 16)
            for i in range(CTX_LOADS):
                t0, t1 = i * FULL // CTX_LOADS, (i + 1) * FULL // CTX_LOADS
                sp.dma_start(ctx_sb[:, t0:t1, :], rows[:, t0:t1, :]).then_inc(ctx_in[i], 16)
            sp.dma_start(ctx_tail[:, :], ctx[0, FULL * P:NK, :]).then_inc(tail_in, 16)
            sp.wait_ge(const_ready, 4)
            for j in range(GH):
                sp.dma_start(wog[QUAD * j:QUAD * j + D, :, :],
                             wo.rearrange("(g j d) n -> j d g n", g=NG, j=GH)[j]).then_inc(wo_in, 16)
            for b in range(PARTS):
                sp.wait_ge(qparts_ready, b + 1)
                sp.dma_start(q_dram[:, b, :, :], qparts[:, b, :]).then_inc(qparts_stored, 16)
            sp.wait_ge(qparts_stored, 16 * PARTS)
            load_q(sp, 0)
            store_k(sp, 0)
            sp.wait_ge(flag_ready, 1)
            safe = sp.value_load(flag[0:1, 0:1], min_val=0, max_val=1)
            with sp.If(safe != 0):
                sp.wait_ge(v_done, VCH)
                sp.wait_ge(pads_ready, 4)
                load_k(sp, 0, 0)
                for s in range(1, NSEG):
                    store_k(sp, s)
                    load_k(sp, 0, s)
                    if s == 2:
                        load_q(sp, 1)
                for g in range(1, NG):
                    for s in range(NSEG):
                        chunks = (s + 1) * SEG_T * NHALF * GH if s < NSEG - 1 else CH_G
                        sp.wait_ge(scores_ready, (g - 1) * TL_G + (chunks - 1) // CPT + 1)
                        load_k(sp, g, s)
                    move_sums(sp, g - 1)
                    if g + 1 < NG:
                        load_q(sp, g + 1)
                move_sums(sp, NG - 1)
            with sp.Else():
                sp.wait_ge(kparts_stored[0], 16 * PARTS)
                sp.wait_ge(qst_in[0], 16 * PARTS * PARTS)
                sp.wait_ge(gfin_ready, 3)
                for h in range(H):
                    j = h % GH
                    sp.dma_start(att[QUAD * j:QUAD * j + D, h // GH, :],
                                 attqT[h * D:(h + 1) * D, :]).then_inc(g_moved, 16)
            sp.wait_ge(topk_ready, 1)
            for e in range(TOPK):
                i = sp.value_load(topi[0:1, e:e + 1], min_val=0, max_val=E - 1)
                sp.dma_start(w1s[:, e, :], w1e[bass.ds(i, 1), :, :].rearrange("e d n -> (e d) n")).then_inc(experts_in, 16)
                sp.dma_start(w2s[:, e, :, :], w2e[bass.ds(i, 1), :, :].rearrange("e (c p) d -> p (e c) d", p=P)).then_inc(experts_in, 16)
                sp.dma_start(b2rows[0:1, 1 + e, :], b2e[bass.ds(i, 1), :]).then_inc(experts_in, 16)
            for n in range(NHALF):
                sp.wait_ge(res_ready, n + 1)
                sp.dma_start(out[0, n * BANK:(n + 1) * BANK, :].rearrange("(t p) c -> p t c", p=P),
                             xn[:, n * QT // 2:(n + 1) * QT // 2, :]).then_inc(out_stored, 16)
            sp.wait_ge(out_stored, 16 * NHALF)

        @block.gpsimd
        def _(pool):
            pool.memset(ident[:, :], 0.0).then_inc(const_zero, 1)
            pool.memset(ones[:, :], 1.0).then_inc(const_ready, 1)
            pool.memset(hmask[:, :], 1.0).then_inc(const_zero, 1)
            pool.wait_ge(const_zero, 1)
            pool.affine_select(out=ident[:, :], in_=ident[:, :], compare_op=ALU.not_equal, fill=1.0, base=0,
                               pattern=[[-1, P]], channel_multiplier=1).then_inc(const_ready, 1)
            pool.wait_ge(const_zero, 2)
            pool.affine_select(out=hmask[:, :], in_=hmask[:, :], compare_op=ALU.is_ge, fill=0.0, base=0,
                               pattern=[[-D, H]], channel_multiplier=1).then_inc(const_zero, 1)
            pool.wait_ge(const_zero, 3)
            pool.affine_select(out=hmask[:, :], in_=hmask[:, :], compare_op=ALU.is_ge, fill=0.0, base=D - 1,
                               pattern=[[D, H]], channel_multiplier=-1).then_inc(const_ready, 1)
            pool.memset(wog[:, :, :], 0.0).then_inc(const_ready, 1)
            pool.wait_ge(const_ready, 4)
            pool.memset(region_ctxT[CK:CK + 1, :], 1.0).then_inc(pads_ready, 1)
            pool.wait_ge(pads_ready, 1)
            pool.memset(tailT[:, :], 0.0).then_inc(pads_ready, 1)
            pool.wait_ge(pads_ready, 2)
            pool.memset(kst[0][:, :, NK:], 0.0).then_inc(pads_ready, 1)
            for dst, src in ((wv_sb[0:CK, :], wv), (wv_sb[CK:CK + 1, :], bv)):
                pool.dma_start(dst, src).then_inc(bo_in, 16)
            for dst, src in ((bsum[0:1, 0, :], bo), (mix[0:1, 3:4], alpha), (wg[:, :], w_gate), (bg[:, :], b_gate),
                             (w1m_sb[:, :], w1m), (w2m_sb[:, :, :], w2m.rearrange("(c p) d -> p c d", p=P)),
                             (b1rows[0:E * CB, :], b1e.rearrange("e (c p) -> (e c) p", p=P)),
                             (b1rows[E * CB:(E + 1) * CB, :], b1m.rearrange("a (c p) -> (a c) p", p=P)),
                             (b2rows[0:1, 0, :], b2m)):
                pool.dma_start(dst, src).then_inc(ffn_in, 16)

        @block.scalar
        def _(act):
            for dst, src in ((wk_sb[:, :], wk), (wq_sb[:, :], wq), (bqc[:, :], bq), (bkc[:, :], bk)):
                act.dma_start(dst, src).then_inc(wts_in, 16)
            act.wait_ge(var_ready, 1)
            act.activation(rstd[:, 1, :], rstd[:, 0, :], ACT.Sqrt).then_inc(std_ready, 1)
            for n in range(NHALF):
                act.wait_ge(xnT_psum, n + 1)
                act.activation(xnT[:, n * BANK:(n + 1) * BANK], po[n][:, :], ACT.Copy).then_inc(xnT_ready, 1)
            act.wait_ge(wts_in, 64)
            for n in range(NHALF):
                act.wait_ge(q_psum, n + 1)
                act.activation(qT[:, n * BANK:(n + 1) * BANK], po[n][:, :], ACT.Identity, bias=bqc[:, 0:1],
                               accum_out=ksum[:, KCH + n:KCH + n + 1]).then_inc(q_ready, 1)
            for c in range(KCH):
                evac_k(act, c)
                if c >= 1:
                    evac_v(act, c - 1)
            evac_v(act, KCH - 1)
            act.wait_ge(flag_ready, 1)
            safe = act.value_load(flag[0:1, 0:1], min_val=0, max_val=1)
            with act.If(safe != 0):
                for t in range(NG * TL_G):
                    act.wait_ge(scores_ready, t + 1)
                    if t >= NPR:
                        g, i = divmod(t - NPR, TL_G)
                        act.wait_ge(pv_done, g * QD_G + step_of(CPT * i + CPT - 1) + 1)
                    act.activation(probs[:, t % NPR, :], ps[t % NSB][:, :], ACT.Exp, scale=SCALE).then_inc(exp_ready, 1)
            with act.Else():
                with act.Fori(0, H) as h:
                    with act.Fori(0, QT) as t:
                        act.wait_ge(gs_shifted, h * QT + t + 1)
                        act.activation(srow[:, :], srow[:, :], ACT.Exp, bias=gen[:, 1:2],
                                       accum_out=gen[:, 2:3]).then_inc(gexp_ready, 1)
            act.wait_ge(var_ready, 2)
            act.activation(rstd[:, 1, :], rstd[:, 0, :], ACT.Sqrt).then_inc(std_ready, 1)
            for n in range(NHALF):
                act.wait_ge(xnT_psum, NHALF + n + 1)
                act.activation(xnT[:, n * BANK:(n + 1) * BANK], ps[1][:, n * BANK:(n + 1) * BANK], ACT.Copy,
                               accum_out=msum[:, n:n + 1]).then_inc(xnT_ready, 1)
            act.wait_ge(msum_ready, 2)
            act.activation(gate[0:1, 2, :], gate[0:1, 1, :], ACT.Exp, accum_out=gate[0:1, 3, 0:1]).then_inc(exp_gate, 1)
            for n in range((1 + TOPK) * CB * NHALF):
                e, r = divmod(n, CB * NHALF)
                cb, half = divmod(r, NHALF)
                act.wait_ge(hid_psum, n + 1)
                if e == 1 and r == 0:
                    act.wait_ge(b1s_ready, 1)
                if e == 2 and r == 0:
                    act.wait_ge(ffn2_done, 1)
                bias = b1T[:, E * CB + cb:E * CB + cb + 1] if e == 0 else b1s[:, e - 1, cb:cb + 1]
                act.activation(hid[e % 2][:, cb, half * BANK:(half + 1) * BANK], bank(n % 6),
                               ACT.Gelu_apprx_tanh, bias=bias).then_inc(hid_ready, 1)

        @block.vector
        def _(dve):
            v = nc.vector

            def chain(step):
                count = [0]

                def link(ins):
                    count[0] += 1
                    ins.then_inc(step, 1)
                    dve.wait_ge(step, count[0])
                return link

            link = chain(dve_step)

            def layernorm(nth, link):
                for t in range(QT):
                    last = v.bn_stats(stats[:, t, :], xres[:, t, :])
                link(last)
                for t in range(QT):
                    last = v.bn_aggr(mv[:, t, :], stats[:, t, :])
                link(last)
                v.tensor_scalar(rstd[:, 0, :], mv[:, :, 1], EPS, None, ALU.add).then_inc(var_ready, 1)
                dve.wait_ge(std_ready, nth)
                link(v.reciprocal(rstd[:, 2, :], rstd[:, 1, :]))
                link(v.tensor_tensor(rstd[:, 3, :], rstd[:, 0, :], rstd[:, 2, :], ALU.mult))
                link(v.tensor_tensor(rstd[:, 2, :], rstd[:, 3, :], rstd[:, 1, :], ALU.add))
                link(v.tensor_scalar(rstd[:, 3, :], rstd[:, 2, :], 0.5, None, ALU.mult))
                link(v.reciprocal(rstd[:, 2, :], rstd[:, 3, :]))
                for t in range(QT):
                    v.tensor_scalar(xn[:, t, :], xres[:, t, :], mv[:, t, 0:1], rstd[:, 2, t:t + 1],
                                    ALU.subtract, ALU.mult).then_inc(xn_ready, 1)

            dve.wait_ge(x_in, 16)
            layernorm(1, link)

            def evac_ctxT(c):
                a, b = c * BANK, min((c + 1) * BANK, NK)
                dve.wait_ge(ctxT_psum, c + 1)
                v.tensor_copy(ctxT[0:CK, a:b], bank(c % 3, CK, b - a)).then_inc(ctxT_ready, 1)

            def range_k(c):
                a, b = c * BANK, min((c + 1) * BANK, NK)
                dve.wait_ge(k_ready, c + 1)
                return v.tensor_reduce(kmax[:, c:c + 1], kT[:, a:b], AX.X, ALU.max, apply_absolute_value=True)

            def split_q():
                dve.wait_ge(q_ready, NHALF)
                v.tensor_copy(qparts[:, 0, :], qT[:, :]).then_inc(qparts_ready, 1)
                dve.wait_ge(qparts_ready, 1)
                link(v.tensor_tensor(q_rest[:, :], qT[:, :], qparts[:, 0, :], ALU.subtract))
                v.tensor_copy(qparts[:, 1, :], q_rest[:, :]).then_inc(qparts_ready, 1)
                dve.wait_ge(qparts_ready, 2)
                v.tensor_tensor(qparts[:, 2, :], q_rest[:, :], qparts[:, 1, :], ALU.subtract).then_inc(qparts_ready, 1)
                dve.wait_ge(xnT_psum, NHALF)
                link(v.tensor_scalar(q_abs[:, :], qT[:, :], -1.0, None, ALU.mult))
                link(v.tensor_tensor(q_abs[:, :], q_abs[:, :], qT[:, :], ALU.max))

            def split_k(s, link):
                a, b = seg_cols(s)
                part, rest = kparts[:, s % 2, :, 0:b - a], krest[:, s % 2, 0:b - a]
                if s >= 2:
                    dve.wait_ge(kparts_stored[s % 2], 16 * PARTS * (s // 2))
                link(v.tensor_copy(part[:, 0, :], kT[:, a:b]))
                link(v.tensor_tensor(rest, kT[:, a:b], part[:, 0, :], ALU.subtract))
                link(v.tensor_copy(part[:, 1, :], rest))
                v.tensor_tensor(part[:, 2, :], rest, part[:, 1, :], ALU.subtract).then_inc(kparts_ready, 1)

            for c in range(KCH):
                evac_ctxT(c)
                if c == 2:
                    split_q()
                if c >= 2:
                    range_k(c - 2)
                if c == 5:
                    split_k(0, link)
            dve.wait_ge(ctxT_ready, KCH)
            dve.wait_ge(pads_ready, 2)
            for j in range(GH):
                last = v.tensor_copy(tailT[:, QUAD * j:QUAD * j + TAIL], ctxT[:, FULL * P:NK])
            last.then_inc(tailT_ready, 1)
            range_k(KCH - 2)
            link(range_k(KCH - 1))
            link(v.tensor_reduce(kcol[:, 0:1], kmax[:, :], AX.X, ALU.max))
            dve.wait_ge(wts_in, 64)
            link(v.tensor_scalar(kcol[:, 1:2], bkc[:, :], -1.0, None, ALU.mult))
            link(v.tensor_tensor(kcol[:, 1:2], kcol[:, 1:2], bkc[:, :], ALU.max))
            link(v.tensor_tensor(kcol[:, 2:3], kcol[:, 1:2], kcol[:, 0:1], ALU.add))
            dve.wait_ge(const_ready, 4)
            v.tensor_scalar(bounds[:, 0:H], hmask[:, :], kcol[:, 0:1], SCALE / SAFE_RANGE, ALU.mult, ALU.mult)
            v.tensor_scalar(bounds[:, H:2 * H], hmask[:, :], kcol[:, 2:3], SCALE / SAFE_SCORE, ALU.mult, ALU.mult).then_inc(bounds_ready, 1)
            link(v.tensor_reduce(kcol[:, 3:4], ksum[:, :], AX.X, ALU.add))
            link(v.tensor_tensor(kcol[:, 5:6], kcol[:, 3:4], bkc[:, :], ALU.add))
            v.tensor_scalar(kcol[:, 4:5], kcol[:, 5:6], 0.0, None, ALU.mult).then_inc(bounds_ready, 1)
            link(v.memset(region_v[:, :], 0.0))
            link(v.memset(vtail[:, :], 0.0))
            for j in range(GH):
                v.memset(vst[:, :, QUAD * j + D:QUAD * j + 2 * D], 1.0)
                last = v.memset(vtail[QUAD * j:QUAD * j + TAIL, QUAD * j + D:QUAD * j + 2 * D], 1.0)
            link(last)
            dve.wait_ge(bound_psum, 1)
            link(v.tensor_reduce(gcol[:, 0:1], ps[0][0:2 * H, 0:NQ], AX.X, ALU.max))
            v.tensor_copy(gcol[:, 1:2], gcol[:, 0:1]).then_inc(gcol_ready, 1)
            dve.wait_ge(grow_psum, 1)
            link(v.tensor_reduce(grow[:, 0:1], ps[0][0:1, 0:2 * H], AX.X, ALU.max))
            link(v.tensor_tensor(grow[:, 1:2], grow[:, 0:1], ps[0][0:1, BANK:BANK + 1], ALU.add))
            v.tensor_scalar(flag[:, :], grow[:, 1:2], 1.0, None, ALU.is_lt).then_inc(flag_ready, 1)
            dve.wait_ge(v_done, VCH)
            v.memset(kst[1][:, :, NK:], 0.0).then_inc(pads_ready, 1)
            dve.wait_ge(rows_psum, 1)
            link(v.tensor_copy(bob[:, :], po[0][:, 0:C]))
            for t in range(QT):
                last = v.tensor_tensor(xres[:, t, :], xres[:, t, :], bob[:, :], ALU.add)
            link(last)
            link(v.tensor_copy(b1T[:, :], po[1][:, 0:(E + 1) * CB]))
            link(v.tensor_scalar(mix[:, 0:1], mix[:, 3:4], 0.1, 1.0, ALU.max, ALU.min))
            v.tensor_scalar(gate[0:1, 7, 0:1], mix[:, 0:1], -1.0, 1.0, ALU.mult, ALU.add).then_inc(rows_taken, 1)
            dve.wait_ge(rows_taken, 1)

            dve.wait_ge(flag_ready, 1)
            safe = dve.value_load(flag[0:1, 0:1], min_val=0, max_val=1)
            with dve.If(safe != 0):
                flink = chain(fast_step)
                def refill(g, s):
                    t0, t1 = s * SEG_T, (s + 1) * SEG_T
                    if g >= 1:
                        dve.wait_ge(pv_done, (g - 1) * QD_G + (t1 * NHALF if s < NSEG - 1 else QD_G))
                    for j in range(GH if s == NSEG - 1 else 0):
                        r = slice(QUAD * j, QUAD * (j + 1))
                        ch = (g * GH + j) * D
                        v.tensor_copy(vtail[r, QUAD * j:QUAD * j + D], vall[r, FULL, ch:ch + D])
                    v.tensor_copy(vst[:, t0:t1, :].rearrange("p t (j m) -> p t j m", j=GH)[:, :, :, 0:D],
                                  vall[:, t0:t1, g * GH * D:(g + 1) * GH * D].rearrange("p t (j d) -> p t j d", j=GH)
                                  ).then_inc(vst_ready, 1)

                refill(0, 0)
                for s in range(1, NSEG):
                    split_k(s, flink)
                    refill(0, s)
                flink(v.memset(oden[:, :], 1.0))
                for g in range(NG):
                    for s in range(NSEG - 1):
                        if g + 1 < NG:
                            refill(g + 1, s)
                    for n in range(NHALF):
                        dve.wait_ge(pv_done, g * QD_G + FULL * NHALF + n + 1)
                        if g >= 1 and n == 0:
                            dve.wait_ge(att_ready, g)
                        v.tensor_copy(oraw[:, n * BANK:(n + 1) * BANK], po[n][:, :]).then_inc(o_taken, 1)
                    if g + 1 < NG:
                        refill(g + 1, NSEG - 1)
                    dve.wait_ge(den_moved, 16 * GH * (g + 1))
                    flink(v.reciprocal(att[:, g, :], oden[:, :]))
                    v.tensor_tensor(att[:, g, :], att[:, g, :], oraw[:, :], ALU.mult
                                    ).then_inc(att_ready if g < NG - 1 else attention_done, 1)
            with dve.Else():
                glink = chain(gen_step)
                glink(v.memset(gen[:, :], 0.0))
                dve.wait_ge(qparts_stored, 16 * PARTS)
                dve.wait_ge(kparts_ready, 1)
                glink(v.tensor_scalar(kT[:, :], kT[:, :], bkc[:, 0:1], None, ALU.add))
                with dve.Fori(0, H) as h:
                    with dve.Fori(0, QT) as t:
                        nth = h * QT + t
                        v.tensor_scalar(qm[:, :], qT[:, bass.ds(t * P, P)], hmask[:, bass.ds(h, 1)], None, ALU.mult).then_inc(gq_ready, 1)
                        for c in range(KCH):
                            a, b = c * BANK, min((c + 1) * BANK, NK)
                            dve.wait_ge(gs_psum, nth * KCH + c + 1)
                            v.tensor_copy(srow[:, a:b], ps[1][:, (c % 2) * BANK:(c % 2) * BANK + b - a]).then_inc(gs_copied, 1)
                        dve.wait_ge(gs_copied, (nth + 1) * KCH)

                        def lstep(ins, n):
                            ins.then_inc(gen_loop_step, 1)
                            dve.wait_ge(gen_loop_step, nth * 8 + n)

                        lstep(v.tensor_tensor(neq[:, :], srow[:, :], srow[:, :], ALU.not_equal), 1)
                        lstep(v.tensor_reduce(gen[:, 3:4], neq[:, :], AX.X, ALU.max), 2)
                        lstep(v.tensor_tensor(gen[:, 0:1], gen[:, 0:1], gen[:, 3:4], ALU.max), 3)
                        lstep(v.tensor_scalar(srow[:, :], srow[:, :], SCALE, CLAMP, ALU.mult, ALU.min), 4)
                        lstep(v.tensor_scalar(srow[:, :], srow[:, :], -CLAMP, None, ALU.max), 5)
                        lstep(v.tensor_reduce(gen[:, 4:5], srow[:, :], AX.X, ALU.max), 6)
                        v.tensor_scalar(gen[:, 1:2], gen[:, 4:5], -1.0, None, ALU.mult).then_inc(gs_shifted, 1)
                        for kt in range(FULL + 1):
                            rows = P if kt < FULL else TAIL
                            dve.wait_ge(gpT_psum, nth * (FULL + 1) + kt + 1)
                            if kt >= 2:
                                dve.wait_ge(go_done, nth * (FULL + 1) + kt - 1)
                            v.tensor_copy(pT[0:rows, kt % 2, :], ps[0][0:rows, (kt % 2) * BANK:(kt % 2) * BANK + P]).then_inc(gpT_ready, 1)
                        dve.wait_ge(go_done, (nth + 1) * (FULL + 1))
                        lstep(v.reciprocal(gen[:, 5:6], gen[:, 2:3]), 7)
                        lstep(v.tensor_scalar(region_v[:, bass.ds(NK // 2 + t * C + h * D, D)], po[0][:, 0:D],
                                              gen[:, 5:6], None, ALU.mult), 8)
                v.tensor_copy(gen[:, 6:7], gen[:, 0:1]).then_inc(gfin_ready, 1)
                dve.wait_ge(gfin_psum, 1)
                glink(v.tensor_scalar(vmean[:, 0, :], po[1][:, 0:C], 1.0 / NK, None, ALU.mult))
                glink(v.tensor_scalar(gen[:, 7:8], po[0][:, 0:1], 0.5, None, ALU.is_gt))
                glink(v.tensor_scalar(vmean[:, 1, :].bitcast(U32), ones[:, :], gen[:, 7:8], None, ALU.mult))
                for t in range(QT):
                    last = v.copy_predicated(attq[:, t, :], vmean[:, 1, :].bitcast(U32), vmean[:, 0, :])
                last.then_inc(gfin_ready, 1)
                dve.wait_ge(gfin_psum, 2)
                glink(v.tensor_copy(attqT[:, :], ps[0][:, 0:NQ]))
                v.memset(region_kT[:, 0:NG * NQ], 0.0).then_inc(gfin_ready, 1)
                dve.wait_ge(g_moved, 16 * H)
                v.memset(gen[:, 7:8], 0.0).then_inc(attention_done, 1)

            tlink = chain(tail_step)
            for n in range(NHALF):
                dve.wait_ge(y_psum, n + 1)
                last = v.tensor_tensor(xres[:, n * QT // 2:(n + 1) * QT // 2, :],
                                       ps[0][:, n * BANK:(n + 1) * BANK].rearrange("p (t c) -> p t c", c=C),
                                       xres[:, n * QT // 2:(n + 1) * QT // 2, :], ALU.add)
            tlink(last)
            layernorm(2, tlink)
            dve.wait_ge(xnT_ready, 2 * NHALF)
            v.tensor_tensor(msum[:, 2:3], msum[:, 0:1], msum[:, 1:2], ALU.add).then_inc(msum_ready, 1)
            dve.wait_ge(logit_psum, 1)
            dve.wait_ge(ffn_in, 16 * FFN_LOADS)
            tlink(v.scalar_tensor_tensor(gate[0:1, 0, :], po[0][0:1, 0:E], 1.0 / NQ, bg[:, :], ALU.mult, ALU.add))
            tlink(v.tensor_reduce(gate[0:1, 4, 0:1], gate[0:1, 0, :], AX.X, ALU.max))
            v.tensor_scalar(gate[0:1, 1, :], gate[0:1, 0, :], gate[0:1, 4, 0:1], None, ALU.subtract).then_inc(msum_ready, 1)
            dve.wait_ge(exp_gate, 1)
            tlink(v.reciprocal(gate[0:1, 4, 1:2], gate[0:1, 3, 0:1]))
            tlink(v.tensor_scalar(gate[0:1, 5, :], gate[0:1, 2, :], gate[0:1, 4, 1:2], None, ALU.mult))
            tlink(v.max(gate[0:1, 6, :], gate[0:1, 5, :]))
            v.max_index(topi[:, :], gate[0:1, 6, :], gate[0:1, 5, :]).then_inc(topk_ready, 1)
            tlink(v.tensor_tensor(gate[0:1, 4, 2:3], gate[0:1, 6, 0:1], gate[0:1, 6, 1:2], ALU.add))
            tlink(v.reciprocal(gate[0:1, 4, 3:4], gate[0:1, 4, 2:3]))
            v.tensor_scalar(mix[0:1, 1:3], gate[0:1, 6, 0:TOPK], gate[0:1, 4, 3:4], gate[0:1, 7, 0:1], ALU.mult, ALU.mult).then_inc(mix_ready, 1)
            dve.wait_ge(topk_ready, 1)
            for e in range(TOPK):
                i = dve.value_load(topi[0:1, e:e + 1], min_val=0, max_val=E - 1)
                last = v.tensor_copy(b1s[:, e, :], b1T[:, bass.ds(i * CB, CB)])
            last.then_inc(b1s_ready, 1)
            dve.wait_ge(mixb_psum, 1)
            tlink(v.tensor_copy(mixb[:, :], po[1][:, 0:3]))
            v.tensor_scalar(w2m_sb[:, :, :], w2m_sb[:, :, :], mixb[:, 0:1], None, ALU.mult).then_inc(w2_scaled, 1)
            dve.wait_ge(experts_in, 16 * 3 * TOPK)
            for e in range(TOPK):
                v.tensor_scalar(w2s[:, e, :, :], w2s[:, e, :, :], mixb[:, 1 + e:2 + e], None, ALU.mult).then_inc(w2_scaled, 1)
            dve.wait_ge(mix_ready, 1)
            tlink(v.tensor_scalar(bsum[0:1, 1, :], b2rows[0:1, 0, :], mix[0:1, 0:1], None, ALU.mult))
            tlink(v.scalar_tensor_tensor(bsum[0:1, 2, :], b2rows[0:1, 1, :], mix[0:1, 1:2], bsum[0:1, 1, :], ALU.mult, ALU.add))
            v.scalar_tensor_tensor(bsum[0:1, 0, :], b2rows[0:1, 2, :], mix[0:1, 2:3], bsum[0:1, 2, :], ALU.mult, ALU.add).then_inc(bsum_ready, 1)
            for n in range(NHALF):
                dve.wait_ge(ffn_psum, n + 1)
                v.tensor_tensor(xn[:, n * QT // 2:(n + 1) * QT // 2, :],
                                po[n][:, :].rearrange("p (t c) -> p t c", c=C),
                                xres[:, n * QT // 2:(n + 1) * QT // 2, :], ALU.add).then_inc(res_ready, 1)

        @block.tensor
        def _(pe):
            mm, tr = nc.tensor.matmul, nc.tensor.transpose
            pe.wait_ge(const_ready, 4)

            def ctx_transpose(c):
                if c >= 3:
                    pe.wait_ge(ctxT_ready, c - 2)
                dst, at = bank(c % 3, CK), 0
                for t in range(4 * c, min(4 * c + 4, FULL)):
                    pe.wait_ge(ctx_in[t * CTX_LOADS // FULL], 16)
                    last = tr(dst[:, at:at + P], ctx_sb[:, t, :], ident[:, :])
                    at += P
                if c == KCH - 1:
                    pe.wait_ge(tail_in, 16)
                    last = tr(dst[:, at:at + TAIL], ctx_tail[:, :], ident[0:TAIL, 0:TAIL])
                last.then_inc(ctxT_psum, 1)

            def project_k(c):
                a, b = c * BANK, min((c + 1) * BANK, NK)
                pe.wait_ge(ctxT_ready, c + 1)
                if c >= 3:
                    pe.wait_ge(k_ready, c - 2)
                mm(bank(3 + c % 3, P, b - a), wk_sb[:, :], ctxT[0:CK, a:b], start=True, stop=True).then_inc(k_psum, 1)

            def project_v(c):
                if c >= 2:
                    pe.wait_ge(v_done, c - 1)
                for t in range(4 * c, min(4 * c + 4, FULL + 1)):
                    if t == FULL:
                        pe.wait_ge(tailT_ready, 1)
                    lhsT = ctxT[:, t * P:(t + 1) * P] if t < FULL else tailT[:, :]
                    last = mm(po[c % 2][:, (t % 4) * P:(t % 4 + 1) * P], lhsT, wv_sb[:, :], start=True, stop=True)
                last.then_inc(v_psum, 1)

            pe.wait_ge(pads_ready, 3)
            ctx_transpose(0)
            ctx_transpose(1)
            for n in range(NHALF):
                for t in range(n * QT // 2, (n + 1) * QT // 2):
                    pe.wait_ge(xn_ready, t + 1)
                    last = tr(po[n][:, (t % 4) * P:(t % 4 + 1) * P], xn[:, t, :], ident[:, :])
                last.then_inc(xnT_psum, 1)
            pe.wait_ge(wts_in, 64)
            for n in range(NHALF):
                pe.wait_ge(xnT_ready, n + 1)
                mm(po[n][:, :], wq_sb[:, :], xnT[:, n * BANK:(n + 1) * BANK], start=True, stop=True).then_inc(q_psum, 1)
            for c in range(KCH):
                if c + 2 < KCH:
                    ctx_transpose(c + 2)
                project_k(c)
                if c == 1:
                    pe.wait_ge(bo_in, 32)
                    pe.wait_ge(q_ready, NHALF)
                if c >= 1:
                    project_v(c - 1)
            pe.wait_ge(bounds_ready, 2)
            for n in range(NHALF):
                last = mm(ps[0][0:2 * H, n * BANK:(n + 1) * BANK], bounds[:, :], q_abs[:, n * BANK:(n + 1) * BANK], start=True, stop=True)
            last.then_inc(bound_psum, 1)
            project_v(KCH - 1)
            pe.wait_ge(gcol_ready, 1)
            mm(ps[0][0:1, 0:2 * H], gcol[:, 1:2], ident[0:2 * H, 0:2 * H], start=True, stop=True)
            mm(ps[0][0:1, BANK:BANK + 1], kcol[:, 4:5], ones[:, 0:1], start=True, stop=True).then_inc(grow_psum, 1)
            pe.wait_ge(ffn_in, 16 * FFN_LOADS)
            pe.wait_ge(v_done, VCH)
            mm(po[0][:, 0:C], ones[0:1, :], bsum[0:1, 0, :], start=True, stop=True)
            tr(po[1][:, 0:(E + 1) * CB], b1rows[:, :], ident[0:(E + 1) * CB, 0:(E + 1) * CB]).then_inc(rows_psum, 1)
            pe.wait_ge(rows_taken, 1)
            pe.wait_ge(flag_ready, 1)
            safe = pe.value_load(flag[0:1, 0:1], min_val=0, max_val=1)
            with pe.If(safe != 0):
                def score_tile(t):
                    g, i = divmod(t, TL_G)
                    if t >= NSB:
                        pe.wait_ge(exp_ready, t - NSB + 1)
                    for m in range(CPT):
                        kt, half, j = chunk(CPT * i + m)
                        if (CPT * i + m) % (SEG_T * NHALF * GH) == 0 and kt < FULL:
                            pe.wait_ge(kst_in[kt // SEG_T], 16 * 2 * PARTS * (g + 1))
                        if CPT * i + m == 0:
                            pe.wait_ge(qst_in[g % 2], 16 * PARTS * PARTS * (g // 2 + 1))
                        queries = slice(half * BANK, (half + 1) * BANK)
                        dst = ps[t % NSB][:, m * BANK:(m + 1) * BANK]
                        for jj in ([j] if kt < FULL else range(GH)):
                            keys, q = kst[jj // 2][0:ROWS, jj % 2, :], qst[:, g % 2, jj, queries]
                            if kt < FULL:
                                last = mm(dst, keys[:, kt * P:(kt + 1) * P], q, start=True, stop=True)
                            else:
                                last = mm(dst[QUAD * jj:QUAD * (jj + 1), :], keys[:, kt * P:kt * P + QUAD], q,
                                          start=True, stop=True, skip_group_check=True)
                    last.then_inc(scores_ready, 1)

                def values_step(g, n):
                    kt, half = divmod(n, NHALF)
                    if half == 0 and kt < FULL and kt % SEG_T == 0:
                        pe.wait_ge(vst_ready, g * NSEG + kt // SEG_T + 1)
                    if g >= 1 and kt == 0:
                        pe.wait_ge(o_taken, (g - 1) * NHALF + half + 1)
                    for j in range(GH if kt < FULL else 1):
                        c = n * GH + j if kt < FULL else FULL * NHALF * GH + half
                        t, m = divmod(c, CPT)
                        src = probs[:, (g * TL_G + t) % NPR, m * BANK:(m + 1) * BANK]
                        if kt < FULL:
                            last = mm(po[half][QUAD * j:QUAD * (j + 1), :], vst[:, kt, QUAD * j:QUAD * (j + 1)], src,
                                      start=(kt == 0), stop=False, skip_group_check=True)
                        else:
                            last = mm(po[half][:, :], vtail[:, :], src, start=False, stop=True, skip_group_check=True)
                    last.then_inc(pv_done, 1)

                for t in range(NSB):
                    score_tile(t)
                for t in range(NG * TL_G):
                    g, i = divmod(t, TL_G)
                    if t + NSB < NG * TL_G:
                        score_tile(t + NSB)
                    else:
                        pe.wait_ge(exp_ready, t + 1)
                    for n in range(QD_G):
                        c = (n + 1) * GH - 1 if n < FULL * NHALF else FULL * NHALF * (GH - 1) + n
                        if c // CPT == i:
                            values_step(g, n)
            with pe.Else():
                with pe.Fori(0, H) as h:
                    with pe.Fori(0, QT) as t:
                        nth = h * QT + t
                        pe.wait_ge(gq_ready, nth + 1)
                        for c in range(KCH):
                            a, b = c * BANK, min((c + 1) * BANK, NK)
                            if c >= 2:
                                pe.wait_ge(gs_copied, nth * KCH + c - 1)
                            mm(ps[1][:, (c % 2) * BANK:(c % 2) * BANK + b - a], qm[:, :], kT[:, a:b], start=True, stop=True).then_inc(gs_psum, 1)
                        pe.wait_ge(gexp_ready, nth + 1)
                        for kt in range(FULL + 1):
                            rows = P if kt < FULL else TAIL
                            if kt >= 2:
                                pe.wait_ge(gpT_ready, nth * (FULL + 1) + kt - 1)
                            tr(ps[0][0:rows, (kt % 2) * BANK:(kt % 2) * BANK + P], srow[:, kt * P:kt * P + rows], ident[:, :]).then_inc(gpT_psum, 1)
                            pe.wait_ge(gpT_ready, nth * (FULL + 1) + kt + 1)
                            mm(po[0][:, 0:D], pT[0:rows, kt % 2, :], vall[0:rows, kt, bass.ds(h * D, D)],
                               start=(kt == 0), stop=(kt == FULL)).then_inc(go_done, 1)
                pe.wait_ge(gfin_ready, 1)
                mm(po[0][:, 0:1], ones[:, :], gen[:, 6:7], start=True, stop=True)
                for kt in range(FULL + 1):
                    rows = P if kt < FULL else TAIL
                    last = mm(po[1][:, 0:C], ones[0:rows, :], vall[0:rows, kt, :], start=(kt == 0), stop=(kt == FULL))
                last.then_inc(gfin_psum, 1)
                pe.wait_ge(gfin_ready, 2)
                for t in range(QT):
                    last = tr(ps[0][:, t * P:(t + 1) * P], attq[:, t, :], ident[:, :])
                last.then_inc(gfin_psum, 1)
            pe.wait_ge(attention_done, 1)
            pe.wait_ge(wo_in, 16 * GH)
            for t in range(QT):
                for g in range(NG):
                    last = mm(ps[0][:, t * P:(t + 1) * P], att[:, g, t * P:(t + 1) * P], wog[:, g, :], start=(g == 0), stop=(g == NG - 1))
                if t % (QT // NHALF) == QT // NHALF - 1:
                    last.then_inc(y_psum, 1)
            for n in range(NHALF):
                for t in range(n * QT // 2, (n + 1) * QT // 2):
                    pe.wait_ge(xn_ready, QT + t + 1)
                    last = tr(ps[1][:, t * P:(t + 1) * P], xn[:, t, :], ident[:, :])
                last.then_inc(xnT_psum, 1)
            pe.wait_ge(msum_ready, 1)
            mm(po[0][0:1, 0:E], msum[:, 2:3], wg[:, :], start=True, stop=True).then_inc(logit_psum, 1)

            def first_layer(e):
                for r in range(CB * NHALF):
                    n = e * CB * NHALF + r
                    cb, half = divmod(r, NHALF)
                    if n >= 6:
                        pe.wait_ge(hid_ready, n - 5)
                    w = w1m_sb[:, cb * P:(cb + 1) * P] if e == 0 else w1s[:, e - 1, cb * P:(cb + 1) * P]
                    mm(bank(n % 6), w,
                       xnT[:, half * BANK:(half + 1) * BANK], start=True, stop=True).then_inc(hid_psum, 1)

            def second_layer(e):
                pe.wait_ge(hid_ready, (e + 1) * CB * NHALF)
                pe.wait_ge(w2_scaled, e + 1)
                if e == TOPK:
                    pe.wait_ge(bsum_ready, 1)
                w2 = w2m_sb if e == 0 else w2s[:, e - 1, :, :]
                for t in range(QT):
                    dst = po[t // 4][:, (t % 4) * P:(t % 4 + 1) * P]
                    for cb in range(CB):
                        last = mm(dst, hid[e % 2][:, cb, t * P:(t + 1) * P], w2[:, cb, :],
                                  start=(e == 0 and cb == 0 and t % 4 == 0), stop=False, skip_group_check=True)
                    if e == TOPK:
                        last = mm(dst, ones[0:1, :], bsum[0:1, 0, :], start=False, stop=True, skip_group_check=True)
                        if t % 4 == 3:
                            last.then_inc(ffn_psum, 1)
                if e < TOPK:
                    last.then_inc(ffn2_done, 1)

            first_layer(0)
            pe.wait_ge(mix_ready, 1)
            mm(po[1][:, 0:3], ones[0:1, :], mix[0:1, 0:3], start=True, stop=True).then_inc(mixb_psum, 1)
            second_layer(0)
            pe.wait_ge(experts_in, 16 * 3 * TOPK)
            first_layer(1)
            first_layer(2)
            second_layer(1)
            second_layer(2)


_OUT = ((1, NQ, C), "float32")


def kernel(x, ctx_768, L0_xattn_Wq, L0_xattn_bq, L0_xattn_Wk, L0_xattn_bk, L0_xattn_Wv, L0_xattn_bv, L0_xattn_Wo,
           L0_xattn_bo, L0_ffn_alpha, L0_ffn_w_gate, L0_ffn_b_gate, L0_ffn_W1m, L0_ffn_b1m, L0_ffn_W2m, L0_ffn_b2m,
           L0_ffn_W1e, L0_ffn_b1e, L0_ffn_W2e, L0_ffn_b2e):
    import numpy as np
    import concourse.bacc as bacc
    from concourse.bass_utils import run_bass_kernel_spmd

    shaped = {
        "x": x, "ctx": ctx_768, "wq": L0_xattn_Wq, "bq": np.reshape(L0_xattn_bq, (C, 1)), "wk": L0_xattn_Wk,
        "bk": np.reshape(L0_xattn_bk, (C, 1)), "wv": L0_xattn_Wv, "bv": np.reshape(L0_xattn_bv, (1, C)),
        "wo": L0_xattn_Wo, "bo": np.reshape(L0_xattn_bo, (1, C)), "alpha": np.reshape(L0_ffn_alpha, (1, 1)),
        "w_gate": L0_ffn_w_gate, "b_gate": np.reshape(L0_ffn_b_gate, (1, E)), "w1m": L0_ffn_W1m,
        "b1m": np.reshape(L0_ffn_b1m, (1, HID)), "w2m": L0_ffn_W2m, "b2m": np.reshape(L0_ffn_b2m, (1, C)),
        "w1e": L0_ffn_W1e, "b1e": L0_ffn_b1e, "w2e": L0_ffn_W2e, "b2e": L0_ffn_b2e,
    }
    nc = bacc.Bacc("TRN2", target_bir_lowering=False, num_devices=1)
    arrays, aps = {}, {}
    for name, value in shaped.items():
        a = np.ascontiguousarray(value)
        arrays[f"in_{name}"] = a
        aps[name] = nc.dram_tensor(f"in_{name}", a.shape, mybir.dt.from_np(a.dtype), kind="ExternalInput").ap()
    shape, dtype = _OUT
    out = nc.dram_tensor("result", shape, mybir.dt.from_np(np.dtype(dtype)), kind="ExternalOutput").ap()
    build(nc, **aps, out=out)
    r = run_bass_kernel_spmd(nc, [arrays], core_ids=[0])
    return r.results[0]["result"]
```

```python
from contextlib import ExitStack

import concourse.bass as bass
from concourse import mybir

F32, BF16, I32, U32 = mybir.dt.float32, mybir.dt.bfloat16, mybir.dt.int32, mybir.dt.uint32
ALU, ACT, AX = mybir.AluOpType, mybir.ActivationFunctionType, mybir.AxisListType

P = 128
NQ, C, CK, NK = 1024, 128, 96, 6404
H, D = 16, 8
E, HID, TOPK = 8, 512, 2
SCALE = float(D) ** -0.5
CLAMP, EPS = 10000.0, 1e-5
SAFE_RANGE = 60.0
SAFE_SCORE = 0.999 * CLAMP

QT = NQ // P
FULL = NK // P
TAIL = NK - FULL * P
BANK = 512
KCH = -(-NK // BANK)
NHALF = NQ // BANK
GH = 4
NG = H // GH
QUAD = P // GH
PARTS = 3
ROWS = PARTS * PARTS * D
SET = PARTS * D
NSEG = 10
SEG_T = FULL // NSEG
SEG_C = SEG_T * P
NSB = 3
CPT = 2
CH_G = FULL * NHALF * GH + NHALF
TL_G = CH_G // CPT
QD_G = FULL * NHALF + NHALF
VCH = -(-(FULL + 1) // 4)
FFN_LOADS = 10
CTX_AT = [0, 4, 12, 24, 37, FULL]
V_ORDER = [0, KCH // 2] + [c for c in range(1, VCH) if c != KCH // 2]
NPR = 4
NORM_AT = 8
BO_BANK = 3 + (KCH - 3) % 3
EARLY_AT, EARLY_GAP = FULL * GH // CPT + 6, 6
FLAG_AHEAD = 3
BOUND_AT = 4
CB = HID // P
MIX_BANK = CB * NHALF % 6
ALPHA_COL = C + (E + 1) * CB
assert CH_G % CPT == 0 and FULL % NSEG == 0


def steps_of(g):
    if g < NG - 1:
        return [(kt, half) for kt in range(FULL + 1) for half in range(NHALF)]
    return [(kt, 0) for kt in range(FULL + 1)] + [(FULL, 1)] + [(kt, 1) for kt in range(FULL)]


def chunks_of(g):
    return [(kt, half, j, n) for n, (kt, half) in enumerate(steps_of(g))
            for j in (range(GH) if kt < FULL else [None])]


STEPS = [steps_of(g) for g in range(NG)]
CHUNKS = [chunks_of(g) for g in range(NG)]


def slot_of_tile(t):
    return t + max(0, (t - NORM_AT) // TL_G)


def slot_of_norm(g):
    return (g + 1) * (TL_G + 1) + NORM_AT - 1


def taker(slot):
    g = max(0, (slot - NORM_AT) // (TL_G + 1))
    return ("norm", g) if slot == slot_of_norm(g) else ("tile", slot - g)


def seg_cols(s):
    return s * SEG_C, (s + 1) * SEG_C if s < NSEG - 1 else NK


def build(nc, x, ctx, wq, bq, wk, bk, wv, bv, wo, bo, alpha, w_gate, b_gate, w1m, b1m, w2m, b2m,
          w1e, b1e, w2e, b2e, out):
    k_dram = nc.dram_tensor("k_dram", (H, PARTS, D, NK), BF16, kind="Internal").ap()
    q_dram = nc.dram_tensor("q_dram", (H, PARTS, D, NQ), BF16, kind="Internal").ap()

    with ExitStack() as stack:
        def sb(name, shape, dt=F32):
            return stack.enter_context(nc.sbuf_tensor(name, shape, dt))

        def sem(name):
            return stack.enter_context(nc.semaphore(name))

        ident = sb("ident", [P, P])
        ones = sb("ones", [P, P])
        hmask = sb("hmask", [P, H])
        xres = sb("xres", [P, QT, C])
        xn = sb("xn", [P, QT, C])
        xnT = sb("xnT", [C, NQ])
        qT = sb("qT", [C, NQ])
        bob = sb("bob", [P, C])
        bqc = sb("bqc", [C, 1])
        bkc = sb("bkc", [C, 1])
        wq_sb = sb("wq_sb", [C, C])
        wk_sb = sb("wk_sb", [CK, C])
        wv_sb = sb("wv_sb", [CK + 1, C])
        wo_sb = sb("wo_sb", [C, C])
        stats = sb("stats", [P, QT, 6])
        mv = sb("mv", [P, QT, 2])
        rstd = sb("rstd", [P, 4, QT])
        region_ctx = sb("region_ctx", [P, FULL * CK])
        ctx_sb = region_ctx[:, :].rearrange("p (t c) -> p t c", t=FULL)
        w1s = region_ctx[:, 0:TOPK * HID].rearrange("p (e n) -> p e n", e=TOPK)
        w2s = region_ctx[:, TOPK * HID:2 * TOPK * HID].rearrange("p (e c n) -> p e c n", e=TOPK, c=CB)
        ctx_tail = sb("ctx_tail", [TAIL, CK])
        region_ctxT = sb("region_ctxT", [P, FULL * P + QUAD])
        ctxT = region_ctxT[0:CK + 1, 0:NK]
        tailT = sb("tailT", [CK + 1, P])
        region_kT = sb("region_kT", [P, NK])
        kT = region_kT
        oraw = region_kT[:, 0:2 * NQ].rearrange("p (b n) -> p b n", b=2)
        rden = sb("rden", [P, QT, GH])
        scratch = sb("scratch", [1, 1])
        kparts = sb("kparts", [P, 2, PARTS, SEG_C + TAIL], BF16)
        krest = sb("krest", [P, 2, SEG_C + TAIL])
        region_k = sb("region_k", [P, FULL * P + QUAD])
        kst = [r[:, :].bitcast(BF16).rearrange("p (w n) -> p w n", w=2) for r in (region_k, region_ctxT)]
        srow = region_k[:, 0:NK]
        vall = sb("vall", [P, FULL + 1, C])
        region_v = sb("region_v", [P, FULL * P])
        vst = region_v[:, :].rearrange("p (t n) -> p t n", t=FULL)
        neq = region_v[:, 0:NK // 2].bitcast(BF16)
        xn_flat = xn[:, :, :].rearrange("p t c -> p (t c)")
        q_abs = xn_flat
        att_tok = xn
        attT = xnT
        free_k = (FULL * P + QUAD) // 2
        q_rest = region_k[:, free_k:free_k + NQ]
        qparts = region_k[:, free_k + NQ:free_k + NQ + PARTS * NQ // 2].bitcast(BF16).rearrange("p (a n) -> p a n", a=PARTS)
        vtail = sb("vtail", [P, P])
        qst = sb("qst", [ROWS, 2, GH, NQ], BF16)
        hid = [region_ctxT[:, 0:CB * NQ].rearrange("p (c n) -> p c n", c=CB),
               region_v[:, 0:CB * NQ].rearrange("p (c n) -> p c n", c=CB)]
        ksum = sb("ksum", [P, KCH + NHALF])
        kmax = sb("kmax", [P, KCH])
        kcol = sb("kcol", [P, 8])
        bounds = sb("bounds", [P, 2 * H])
        gcol = sb("gcol", [2 * H, NHALF + 1])
        grow = sb("grow", [1, 4])
        flag = sb("flag", [1, 1], I32)
        w1m_sb = sb("w1m_sb", [C, HID])
        w2m_sb = sb("w2m_sb", [P, CB, C])
        b1rows = sb("b1rows", [(E + 1) * CB, P])
        b1T = sb("b1T", [P, (E + 1) * CB])
        b1s = sb("b1s", [P, TOPK, CB])
        b2rows = sb("b2rows", [1, 3, C])
        wg = sb("wg", [C, E])
        bg = sb("bg", [1, E])
        msum = sb("msum", [C, 4])
        gate = sb("gate", [1, 12, E])
        topi = sb("topi", [1, 8], U32)
        mix = sb("mix", [1, 4])
        mixb = sb("mixb", [P, 3])
        bsum = sb("bsum", [1, 3, C])
        qm = sb("qm", [C, P])
        pT = sb("pT", [P, 2, P])
        gen = sb("gen", [P, 8])
        vmean = sb("vmean", [P, 2, C])

        probs = region_ctx[:, 0:NPR * CPT * BANK].rearrange("p (b n) -> p b n", b=NPR)

        ps = [stack.enter_context(nc.psum_tensor(f"ps{i}", [P, CPT * BANK], F32)) for i in range(NSB)]
        po = [stack.enter_context(nc.psum_tensor(f"po{i}", [P, BANK], F32)) for i in range(NHALF)]

        def bank(i, rows=P, cols=BANK):
            return ps[i // CPT][0:rows, i % CPT * BANK:i % CPT * BANK + cols]

        x_in, wk_in, wts_in, wv_in, tail_in, ffn_in = (sem(n) for n in ("x_in", "wk_in", "wts_in", "wv_in", "tail_in", "ffn_in"))
        ctx_in = [sem(f"ctx_in{i}") for i in range(len(CTX_AT) - 1)]
        const_zero, const_ready, pads_ready, vones_ready = sem("const_zero"), sem("const_ready"), sem("pads_ready"), sem("vones_ready")
        dve_step, fast_step, gen_step, gen_loop_step, tail_step = (sem(n) for n in ("dve_step", "fast_step", "gen_step", "gen_loop_step", "tail_step"))
        var_ready, std_ready, xn_ready = sem("var_ready"), sem("std_ready"), sem("xn_ready")
        xnT_psum, xnT_ready, q_psum, q_ready = sem("xnT_psum"), sem("xnT_ready"), sem("q_psum"), sem("q_ready")
        ctxT_psum, ctxT_ready, tailT_ready = sem("ctxT_psum"), sem("ctxT_ready"), sem("tailT_ready")
        k_psum, k_ready, v_psum, v_done = sem("k_psum"), sem("k_ready"), sem("v_psum"), sem("v_done")
        kparts_ready = sem("kparts_ready")
        kparts_stored = [sem("kparts_stored0"), sem("kparts_stored1")]
        qparts_ready, qparts_stored = sem("qparts_ready"), sem("qparts_stored")
        qst_in = [sem("qst_in0"), sem("qst_in1")]
        q_abs_ready = sem("q_abs_ready")
        bounds_ready, bound_psum, gcol_ready, grow_psum, flag_ready = (sem(n) for n in ("bounds_ready", "bound_psum", "gcol_ready", "grow_psum", "flag_ready"))
        kst_in = [sem(f"kst_in{s}") for s in range(NSEG)]
        vst_ready = sem("vst_ready")
        scores_ready, exp_ready, pv_done, o_taken = sem("scores_ready"), sem("exp_ready"), sem("pv_done"), sem("o_taken")
        tok_psum, tok_taken = sem("tok_psum"), sem("tok_taken")
        table_step = sem("table_step")
        rows_psum, attention_done = sem("rows_psum"), sem("attention_done")
        attT_psum, attT_ready = sem("attT_psum"), sem("attT_ready")
        gq_ready, gs_psum, gs_copied, gs_shifted, gexp_ready, gpT_psum, gpT_ready, go_done, gfin_psum, gfin_ready = (
            sem(n) for n in ("gq_ready", "gs_psum", "gs_copied", "gs_shifted", "gexp_ready", "gpT_psum", "gpT_ready", "go_done", "gfin_psum", "gfin_ready"))
        y_psum, y_taken, logit_psum, exp_gate, topk_ready, mix_ready, mixb_psum, mixb_taken = (
            sem(n) for n in ("y_psum", "y_taken", "logit_psum", "exp_gate", "topk_ready", "mix_ready", "mixb_psum", "mixb_taken"))
        experts_in, w2_scaled, hid_psum, hid_ready, ffn2_done, bsum_ready, b1s_ready, rows_taken = (
            sem(n) for n in ("experts_in", "w2_scaled", "hid_psum", "hid_ready", "ffn2_done", "bsum_ready", "b1s_ready", "rows_taken"))
        msum_ready, ffn_psum, res_ready, out_stored = sem("msum_ready"), sem("ffn_psum"), sem("res_ready"), sem("out_stored")

        block = stack.enter_context(nc.Block())

        def store_k(sp, s):
            a, b = seg_cols(s)
            sp.wait_ge(kparts_ready, s + 1)
            for part in range(PARTS):
                sp.dma_start(k_dram[:, part, :, a:b],
                             kparts[:, s % 2, part, 0:b - a]).then_inc(kparts_stored[s % 2], 16)

        def load_k(sp, g, s):
            a, b = seg_cols(s)
            if g == 0:
                sp.wait_ge(kparts_stored[s % 2], 16 * PARTS * (s // 2 + 1))
            for r in range(2):
                rows = k_dram[GH * g + 2 * r:GH * g + 2 * r + 2, :, :, a:b].rearrange("w a d n -> (a d) w n")
                for m in range(PARTS):
                    sp.dma_start(kst[r][SET * m:SET * (m + 1), :, a:b], rows).then_inc(kst_in[s], 16)

        def load_q(sp, g):
            if g >= 2:
                sp.wait_ge(scores_ready, (g - 1) * TL_G)
            for m in range(PARTS):
                rows = q_dram[GH * g:GH * (g + 1), m, :, :].rearrange("w d n -> d w n")
                for a in range(PARTS):
                    sp.dma_start(qst[SET * m + D * a:SET * m + D * (a + 1), g % 2, :, :], rows).then_inc(qst_in[g % 2], 16)

        def evac_ctxT(act, c):
            a, b = c * BANK, min((c + 1) * BANK, NK)
            act.wait_ge(ctxT_psum, c + 1)
            act.activation(ctxT[0:CK, a:b], bank(c % 3, CK, b - a), ACT.Copy).then_inc(ctxT_ready, 1)

        def evac_k(act, c):
            a, b = c * BANK, min((c + 1) * BANK, NK)
            act.wait_ge(k_psum, c + 1)
            act.activation(kT[:, a:b], bank(3 + c % 3, P, b - a), ACT.Copy,
                           accum_out=ksum[:, c:c + 1]).then_inc(k_ready, 1)

        def evac_v(act, nth):
            c = V_ORDER[nth]
            n = min(4, FULL + 1 - 4 * c)
            act.wait_ge(v_psum, nth + 1)
            act.activation(vall[:, 4 * c:4 * c + n, :].rearrange("p t n -> p (t n)"), po[nth % 2][:, 0:n * P], ACT.Copy).then_inc(v_done, 1)

        @block.sync
        def _(sp):
            rows = ctx[0, 0:FULL * P, :].rearrange("(p t) c -> p t c", t=FULL)
            for i, (t0, t1) in enumerate(zip(CTX_AT[:-1], CTX_AT[1:])):
                sp.dma_start(ctx_sb[:, t0:t1, :], rows[:, t0:t1, :]).then_inc(ctx_in[i], 16)
                if i == 0:
                    sp.dma_start(xres[:, :, :], x[0].rearrange("(t p) c -> p t c", p=P)).then_inc(x_in, 16)
            sp.dma_start(ctx_tail[:, :], ctx[0, FULL * P:NK, :]).then_inc(tail_in, 16)
            for b in range(PARTS):
                sp.wait_ge(qparts_ready, b + 1)
                sp.dma_start(q_dram[:, b, :, :], qparts[:, b, :]).then_inc(qparts_stored, 16)
            sp.wait_ge(qparts_stored, 16 * PARTS)
            load_q(sp, 0)
            store_k(sp, 0)
            sp.wait_ge(v_done, 2)
            load_k(sp, 0, 0)
            sp.wait_ge(flag_ready, 1)
            safe = sp.value_load(flag[0:1, 0:1], min_val=0, max_val=1)
            with sp.If(safe != 0):
                sp.wait_ge(v_done, VCH)
                sp.wait_ge(pads_ready, 4)
                for s in range(1, NSEG):
                    store_k(sp, s)
                    load_k(sp, 0, s)
                    if s == 2:
                        load_q(sp, 1)
                for g in range(1, NG):
                    for s in range(NSEG):
                        chunks = (s + 1) * SEG_T * NHALF * GH if s < NSEG - 1 else CH_G
                        sp.wait_ge(scores_ready, (g - 1) * TL_G + (chunks - 1) // CPT + 1)
                        load_k(sp, g, s)
                    if g + 1 < NG:
                        load_q(sp, g + 1)
            with sp.Else():
                sp.wait_ge(kst_in[0], 16 * 2 * PARTS)
                sp.wait_ge(qst_in[0], 16 * PARTS * PARTS)
            sp.wait_ge(topk_ready, 1)
            for e in range(TOPK):
                i = sp.value_load(topi[0:1, e:e + 1], min_val=0, max_val=E - 1)
                sp.dma_start(w1s[:, e, :], w1e[bass.ds(i, 1), :, :].rearrange("e d n -> (e d) n")).then_inc(experts_in, 16)
                sp.dma_start(w2s[:, e, :, :], w2e[bass.ds(i, 1), :, :].rearrange("e (c p) d -> p (e c) d", p=P)).then_inc(experts_in, 16)
                sp.dma_start(b2rows[0:1, 1 + e, :], b2e[bass.ds(i, 1), :]).then_inc(experts_in, 16)
            for n in range(NHALF):
                sp.wait_ge(res_ready, n + 1)
                sp.dma_start(out[0, n * BANK:(n + 1) * BANK, :].rearrange("(t p) c -> p t c", p=P),
                             xn[:, n * QT // 2:(n + 1) * QT // 2, :]).then_inc(out_stored, 16)
            sp.wait_ge(out_stored, 16 * NHALF)

        @block.gpsimd
        def _(pool):
            pool.memset(ident[:, :], 0.0).then_inc(const_zero, 1)
            pool.memset(ones[:, :], 1.0).then_inc(const_ready, 1)
            pool.memset(hmask[:, :], 1.0).then_inc(const_zero, 1)
            pool.wait_ge(const_zero, 1)
            pool.affine_select(out=ident[:, :], in_=ident[:, :], compare_op=ALU.not_equal, fill=1.0, base=0,
                               pattern=[[-1, P]], channel_multiplier=1).then_inc(const_ready, 1)
            pool.wait_ge(const_zero, 2)
            pool.affine_select(out=hmask[:, :], in_=hmask[:, :], compare_op=ALU.is_ge, fill=0.0, base=0,
                               pattern=[[-D, H]], channel_multiplier=1).then_inc(const_zero, 1)
            pool.wait_ge(const_zero, 3)
            pool.affine_select(out=hmask[:, :], in_=hmask[:, :], compare_op=ALU.is_ge, fill=0.0, base=D - 1,
                               pattern=[[D, H]], channel_multiplier=-1).then_inc(const_ready, 1)
            pool.wait_ge(const_ready, 3)
            pool.memset(region_ctxT[CK:CK + 1, :], 1.0).then_inc(pads_ready, 1)
            pool.wait_ge(pads_ready, 1)
            pool.memset(tailT[:, :], 0.0).then_inc(pads_ready, 1)
            pool.wait_ge(pads_ready, 2)
            pool.memset(kst[0][:, :, NK:], 0.0).then_inc(pads_ready, 1)
            for dst, src in ((wv_sb[0:CK, :], wv), (wv_sb[CK:CK + 1, :], bv)):
                pool.dma_start(dst, src).then_inc(wv_in, 16)
            for dst, src in ((bsum[0:1, 0, :], bo), (wo_sb[:, :], wo), (mix[0:1, 3:4], alpha), (wg[:, :], w_gate), (bg[:, :], b_gate),
                             (w1m_sb[:, :], w1m), (w2m_sb[:, :, :], w2m.rearrange("(c p) d -> p c d", p=P)),
                             (b1rows[0:E * CB, :], b1e.rearrange("e (c p) -> (e c) p", p=P)),
                             (b1rows[E * CB:(E + 1) * CB, :], b1m.rearrange("a (c p) -> (a c) p", p=P)),
                             (b2rows[0:1, 0, :], b2m)):
                pool.dma_start(dst, src).then_inc(ffn_in, 16)
            pool.memset(region_v[:, :], 0.0).then_inc(vones_ready, 1)
            pool.wait_ge(vones_ready, 1)
            pool.memset(vtail[:, :], 0.0).then_inc(vones_ready, 1)
            for j in range(GH):
                pool.wait_ge(vones_ready, 2 + 2 * j)
                pool.memset(vst[:, :, QUAD * j + D:QUAD * j + 2 * D], 1.0).then_inc(vones_ready, 1)
                pool.wait_ge(vones_ready, 3 + 2 * j)
                pool.memset(vtail[QUAD * j:QUAD * j + TAIL, QUAD * j + D:QUAD * j + 2 * D], 1.0).then_inc(vones_ready, 1)

        @block.scalar
        def _(act):
            act.dma_start(wk_sb[:, :], wk).then_inc(wk_in, 16)
            for dst, src in ((wq_sb[:, :], wq), (bqc[:, :], bq), (bkc[:, :], bk)):
                act.dma_start(dst, src).then_inc(wts_in, 16)
            evac_ctxT(act, 0)
            evac_ctxT(act, 1)
            act.wait_ge(var_ready, 1)
            act.activation(rstd[:, 1, :], rstd[:, 0, :], ACT.Sqrt).then_inc(std_ready, 1)
            evac_ctxT(act, 2)
            evac_k(act, 0)
            evac_ctxT(act, 3)
            evac_k(act, 1)
            evac_ctxT(act, 4)
            evac_k(act, 2)
            act.wait_ge(wts_in, 48)
            for n in range(NHALF):
                act.wait_ge(q_psum, n + 1)
                act.activation(qT[:, n * BANK:(n + 1) * BANK], po[n][:, :], ACT.Identity, bias=bqc[:, 0:1],
                               accum_out=ksum[:, KCH + n:KCH + n + 1]).then_inc(q_ready, 1)
                act.activation(q_abs[:, n * BANK:(n + 1) * BANK], po[n][:, :], ACT.Abs, bias=bqc[:, 0:1]).then_inc(q_abs_ready, 1)
            for c in range(3, KCH):
                if c + 2 < KCH:
                    evac_ctxT(act, c + 2)
                evac_k(act, c)
            for nth in range(VCH):
                if nth == VCH - FLAG_AHEAD:
                    act.wait_ge(flag_ready, 1)
                    safe = act.value_load(flag[0:1, 0:1], min_val=0, max_val=1)
                    act.activation(scratch[:, :], ones[0:1, 0:1], ACT.Exp).then_inc(table_step, 1)
                evac_v(act, nth)
            with act.If(safe != 0):
                for t in range(NG * TL_G):
                    act.wait_ge(scores_ready, t + 1)
                    if t >= NPR:
                        g, i = divmod(t - NPR, TL_G)
                        act.wait_ge(pv_done, g * QD_G + CHUNKS[g][CPT * i + CPT - 1][3] + 1)
                    act.activation(probs[:, t % NPR, :], ps[slot_of_tile(t) % NSB][:, :], ACT.Exp, scale=SCALE).then_inc(exp_ready, 1)
            with act.Else():
                with act.Fori(0, H) as h:
                    with act.Fori(0, QT) as t:
                        act.wait_ge(gs_shifted, h * QT + t + 1)
                        act.activation(srow[:, :], srow[:, :], ACT.Exp, bias=gen[:, 1:2],
                                       accum_out=gen[:, 2:3]).then_inc(gexp_ready, 1)
            act.wait_ge(var_ready, 2)
            act.activation(rstd[:, 1, 0:QT // 2], rstd[:, 0, 0:QT // 2], ACT.Sqrt).then_inc(std_ready, 1)
            act.wait_ge(attT_psum, NHALF)
            act.activation(attT[:, BANK:NQ], bank(4), ACT.Copy).then_inc(attT_ready, 1)

            def take_xnT(n):
                act.wait_ge(xnT_psum, NHALF + n + 1)
                act.activation(xnT[:, n * BANK:(n + 1) * BANK], po[n][:, :], ACT.Copy,
                               accum_out=msum[:, n:n + 1]).then_inc(xnT_ready, 1)

            def hidden(n):
                e, r = divmod(n, CB * NHALF)
                half, cb = divmod(r, CB)
                act.wait_ge(hid_psum, n + 1)
                if e == 1 and r == 0:
                    act.wait_ge(b1s_ready, 1)
                if e == 2 and r == 0:
                    act.wait_ge(ffn2_done, 1)
                bias = b1T[:, E * CB + cb:E * CB + cb + 1] if e == 0 else b1s[:, e - 1, cb:cb + 1]
                act.activation(hid[e % 2][:, cb, half * BANK:(half + 1) * BANK], bank(n % 6),
                               ACT.Gelu_apprx_tanh, bias=bias).then_inc(hid_ready, 1)

            take_xnT(0)
            act.wait_ge(var_ready, 3)
            act.activation(rstd[:, 1, QT // 2:QT], rstd[:, 0, QT // 2:QT], ACT.Sqrt).then_inc(std_ready, 1)
            hidden(0)
            hidden(1)
            take_xnT(1)
            hidden(2)
            hidden(3)
            act.wait_ge(msum_ready, 2)
            act.activation(gate[0:1, 2, :], gate[0:1, 1, :], ACT.Exp, accum_out=gate[0:1, 3, 0:1]).then_inc(exp_gate, 1)
            for n in range(CB, (1 + TOPK) * CB * NHALF):
                hidden(n)

        @block.vector
        def _(dve):
            v = nc.vector

            def chain(step):
                count = [0]

                def link(ins):
                    count[0] += 1
                    ins.then_inc(step, 1)
                    dve.wait_ge(step, count[0])
                return link

            link = chain(dve_step)

            def statistics(tiles, link):
                for t in tiles:
                    last = v.bn_stats(stats[:, t, :], xres[:, t, :])
                link(last)
                for t in tiles:
                    last = v.bn_aggr(mv[:, t, :], stats[:, t, :])
                link(last)
                r = slice(tiles.start, tiles.stop)
                v.tensor_scalar(rstd[:, 0, r], mv[:, r, 1], EPS, 0.25, ALU.add, ALU.mult).then_inc(var_ready, 1)

            def layernorm(nth, tiles, link):
                r = slice(tiles.start, tiles.stop)
                dve.wait_ge(std_ready, nth)
                link(v.reciprocal(rstd[:, 2, r], rstd[:, 1, r]))
                link(v.tensor_tensor(rstd[:, 3, r], rstd[:, 0, r], rstd[:, 2, r], ALU.mult))
                link(v.tensor_tensor(rstd[:, 2, r], rstd[:, 3, r], rstd[:, 1, r], ALU.add))
                link(v.reciprocal(rstd[:, 3, r], rstd[:, 2, r]))
                for t in tiles:
                    v.tensor_scalar(xn[:, t, :], xres[:, t, :], mv[:, t, 0:1], rstd[:, 3, t:t + 1],
                                    ALU.subtract, ALU.mult).then_inc(xn_ready, 1)

            dve.wait_ge(x_in, 16)
            statistics(range(QT), link)
            layernorm(1, range(QT), link)
            for n in range(NHALF):
                dve.wait_ge(xnT_psum, n + 1)
                v.tensor_copy(xnT[:, n * BANK:(n + 1) * BANK], po[n][:, :]).then_inc(xnT_ready, 1)

            def range_k(c):
                a, b = c * BANK, min((c + 1) * BANK, NK)
                dve.wait_ge(k_ready, c + 1)
                return v.tensor_reduce(kmax[:, c:c + 1], kT[:, a:b], AX.X, ALU.max, apply_absolute_value=True)

            def split_q():
                dve.wait_ge(q_ready, NHALF)
                v.tensor_copy(qparts[:, 0, :], qT[:, :]).then_inc(qparts_ready, 1)
                dve.wait_ge(qparts_ready, 1)
                link(v.tensor_tensor(q_rest[:, :], qT[:, :], qparts[:, 0, :], ALU.subtract))
                v.tensor_copy(qparts[:, 1, :], q_rest[:, :]).then_inc(qparts_ready, 1)
                dve.wait_ge(qparts_ready, 2)
                v.tensor_tensor(qparts[:, 2, :], q_rest[:, :], qparts[:, 1, :], ALU.subtract).then_inc(qparts_ready, 1)

            def split_k(s, link):
                a, b = seg_cols(s)
                part, rest = kparts[:, s % 2, :, 0:b - a], krest[:, s % 2, 0:b - a]
                if s >= 2:
                    dve.wait_ge(kparts_stored[s % 2], 16 * PARTS * (s // 2))
                link(v.tensor_copy(part[:, 0, :], kT[:, a:b]))
                link(v.tensor_tensor(rest, kT[:, a:b], part[:, 0, :], ALU.subtract))
                link(v.tensor_copy(part[:, 1, :], rest))
                v.tensor_tensor(part[:, 2, :], rest, part[:, 1, :], ALU.subtract).then_inc(kparts_ready, 1)

            for c in range(KCH - 1):
                if c == 1:
                    split_q()
                range_k(c)
                if c == 4:
                    split_k(0, link)
            dve.wait_ge(ctxT_ready, KCH)
            dve.wait_ge(pads_ready, 2)
            for j in range(GH):
                last = v.tensor_copy(tailT[:, QUAD * j:QUAD * j + TAIL], ctxT[:, FULL * P:NK])
            last.then_inc(tailT_ready, 1)
            link(range_k(KCH - 1))
            link(v.tensor_reduce(kcol[:, 0:1], kmax[:, :], AX.X, ALU.max))
            dve.wait_ge(wts_in, 48)
            link(v.tensor_scalar(kcol[:, 1:2], bkc[:, :], -1.0, None, ALU.mult))
            link(v.tensor_tensor(kcol[:, 1:2], kcol[:, 1:2], bkc[:, :], ALU.max))
            link(v.tensor_tensor(kcol[:, 2:3], kcol[:, 1:2], kcol[:, 0:1], ALU.add))
            dve.wait_ge(const_ready, 3)
            v.tensor_scalar(bounds[:, 0:H], hmask[:, :], kcol[:, 0:1], SCALE / SAFE_RANGE, ALU.mult, ALU.mult)
            v.tensor_scalar(bounds[:, H:2 * H], hmask[:, :], kcol[:, 2:3], SCALE / SAFE_SCORE, ALU.mult, ALU.mult).then_inc(bounds_ready, 1)
            link(v.tensor_reduce(kcol[:, 3:4], ksum[:, :], AX.X, ALU.add))
            link(v.tensor_tensor(kcol[:, 5:6], kcol[:, 3:4], bkc[:, :], ALU.add))
            v.tensor_scalar(kcol[:, 4:5], kcol[:, 5:6], 0.0, None, ALU.mult).then_inc(bounds_ready, 1)
            dve.wait_ge(rows_psum, 1)
            v.tensor_copy(bob[:, :], bank(BO_BANK)[:, 0:C])
            v.tensor_scalar(mixb[:, 0:1], bank(BO_BANK)[:, ALPHA_COL:ALPHA_COL + 1], 0.1, 1.0, ALU.max, ALU.min)
            v.tensor_copy(b1T[:, :], bank(BO_BANK)[:, C:C + (E + 1) * CB]).then_inc(rows_taken, 1)
            link(v.tensor_scalar(mix[:, 0:1], mix[:, 3:4], 0.1, 1.0, ALU.max, ALU.min))
            link(v.tensor_scalar(gate[0:1, 7, 0:1], mix[:, 0:1], -1.0, 1.0, ALU.mult, ALU.add))
            dve.wait_ge(bound_psum, 1)
            link(v.tensor_reduce(gcol[:, 0:1], ps[0][0:2 * H, 0:NQ], AX.X, ALU.max))
            v.tensor_copy(gcol[:, 1:2], gcol[:, 0:1]).then_inc(gcol_ready, 1)
            dve.wait_ge(grow_psum, 1)
            link(v.tensor_reduce(grow[:, 0:1], ps[0][0:1, 0:2 * H], AX.X, ALU.max))
            link(v.tensor_tensor(grow[:, 1:2], grow[:, 0:1], ps[0][0:1, BANK:BANK + 1], ALU.add))
            v.tensor_scalar(flag[:, :], grow[:, 1:2], 1.0, None, ALU.is_lt).then_inc(flag_ready, 1)

            halves = [range(n * QT // 2, (n + 1) * QT // 2) for n in range(NHALF)]

            def residual(n, y, link):
                r = slice(halves[n].start, halves[n].stop)
                dve.wait_ge(y_psum, n + 1)
                v.tensor_tensor(xres[:, r, :], y.rearrange("p (t c) -> p t c", c=C), xres[:, r, :], ALU.add).then_inc(y_taken, 1)
                dve.wait_ge(y_taken, n + 1)
                statistics(halves[n], link)

            def take_first_attT():
                dve.wait_ge(attT_psum, 1)
                v.tensor_copy(attT[:, 0:BANK], po[0][:, :]).then_inc(attT_ready, 1)

            def add_bo(link):
                dve.wait_ge(rows_taken, 1)
                v.tensor_scalar(w2m_sb[:, :, :], w2m_sb[:, :, :], mixb[:, 0:1], None, ALU.mult).then_inc(w2_scaled, 1)
                for t in range(QT):
                    last = v.tensor_tensor(xres[:, t, :], xres[:, t, :], bob[:, :], ALU.add)
                link(last)

            dve.wait_ge(flag_ready, 1)
            safe = dve.value_load(flag[0:1, 0:1], min_val=0, max_val=1)
            with dve.If(safe != 0):
                flink = chain(fast_step)
                def refill(g, s):
                    t0, t1 = s * SEG_T, (s + 1) * SEG_T
                    if g >= 1:
                        dve.wait_ge(pv_done, (g - 1) * QD_G + (t1 * NHALF if s < NSEG - 1 else QD_G))
                    for j in range(GH if s == NSEG - 1 else 0):
                        r = slice(QUAD * j, QUAD * (j + 1))
                        ch = (g * GH + j) * D
                        v.tensor_copy(vtail[r, QUAD * j:QUAD * j + D], vall[r, FULL, ch:ch + D])
                    v.tensor_copy(vst[:, t0:t1, :].rearrange("p t (j m) -> p t j m", j=GH)[:, :, :, 0:D],
                                  vall[:, t0:t1, g * GH * D:(g + 1) * GH * D].rearrange("p t (j d) -> p t j d", j=GH)
                                  ).then_inc(vst_ready, 1)

                dve.wait_ge(vones_ready, 2 + 2 * GH)
                dve.wait_ge(v_done, 3)
                refill(0, 0)
                for s in range(1, NSEG):
                    split_k(s, flink)
                    if s == 1:
                        dve.wait_ge(v_done, VCH)
                        v.memset(kst[1][:, :, NK:], 0.0).then_inc(pads_ready, 1)
                    refill(0, s)
                add_bo(flink)

                def normalise(g, tok, tiles):
                    tok4 = tok.rearrange("p (t j m) -> p t j m", j=GH, m=QUAD)
                    n = tiles.stop - tiles.start
                    flink(v.reciprocal(rden[:, tiles, :], tok4[:, :, :, D]))
                    return v.tensor_tensor(att_tok[:, tiles, g * GH * D:(g + 1) * GH * D].rearrange("p t (j d) -> p t j d", j=GH),
                                           tok4[:, :, :, 0:D],
                                           rden[:, tiles, :].unsqueeze(3).broadcast_to([P, n, GH, D]), ALU.mult)

                for g in range(NG - 1):
                    for s in range(NSEG - 1):
                        refill(g + 1, s)
                    for n in range(NHALF):
                        dve.wait_ge(pv_done, g * QD_G + FULL * NHALF + n + 1)
                        v.tensor_copy(oraw[:, g % 2, n * BANK:(n + 1) * BANK], po[n][:, :]).then_inc(o_taken, 1)
                    refill(g + 1, NSEG - 1)
                    dve.wait_ge(tok_psum, g + 1)
                    normalise(g, ps[slot_of_norm(g) % NSB][:, :], slice(0, QT)).then_inc(tok_taken, 1)
                for n in range(NHALF):
                    dve.wait_ge(pv_done, (NG - 1) * QD_G + max(i for i, (_, half) in enumerate(STEPS[NG - 1]) if half == n) + 1)
                    v.tensor_copy(oraw[:, (NG - 1) % 2, n * BANK:(n + 1) * BANK], po[n][:, :]).then_inc(o_taken, 1)
                    dve.wait_ge(tok_psum, NG + n)
                    normalise(NG - 1, po[0][:, :], slice(halves[n].start, halves[n].stop)).then_inc(attention_done, 1)
                    if n == 0:
                        take_first_attT()
                        residual(0, po[0][:, :], flink)
            with dve.Else():
                glink = chain(gen_step)
                glink(v.memset(gen[:, :], 0.0))
                dve.wait_ge(vones_ready, 2 + 2 * GH)
                dve.wait_ge(kst_in[0], 16 * 2 * PARTS)
                dve.wait_ge(v_done, VCH)
                add_bo(glink)
                glink(v.tensor_scalar(kT[:, :], kT[:, :], bkc[:, 0:1], None, ALU.add))
                with dve.Fori(0, H) as h:
                    with dve.Fori(0, QT) as t:
                        nth = h * QT + t
                        v.tensor_scalar(qm[:, :], qT[:, bass.ds(t * P, P)], hmask[:, bass.ds(h, 1)], None, ALU.mult).then_inc(gq_ready, 1)
                        for c in range(KCH):
                            a, b = c * BANK, min((c + 1) * BANK, NK)
                            dve.wait_ge(gs_psum, nth * KCH + c + 1)
                            v.tensor_copy(srow[:, a:b], ps[1][:, (c % 2) * BANK:(c % 2) * BANK + b - a]).then_inc(gs_copied, 1)
                        dve.wait_ge(gs_copied, (nth + 1) * KCH)

                        def lstep(ins, n):
                            ins.then_inc(gen_loop_step, 1)
                            dve.wait_ge(gen_loop_step, nth * 8 + n)

                        lstep(v.tensor_tensor(neq[:, :], srow[:, :], srow[:, :], ALU.not_equal), 1)
                        lstep(v.tensor_reduce(gen[:, 3:4], neq[:, :], AX.X, ALU.max), 2)
                        lstep(v.tensor_tensor(gen[:, 0:1], gen[:, 0:1], gen[:, 3:4], ALU.max), 3)
                        lstep(v.tensor_scalar(srow[:, :], srow[:, :], SCALE, CLAMP, ALU.mult, ALU.min), 4)
                        lstep(v.tensor_scalar(srow[:, :], srow[:, :], -CLAMP, None, ALU.max), 5)
                        lstep(v.tensor_reduce(gen[:, 4:5], srow[:, :], AX.X, ALU.max), 6)
                        v.tensor_scalar(gen[:, 1:2], gen[:, 4:5], -1.0, None, ALU.mult).then_inc(gs_shifted, 1)
                        for kt in range(FULL + 1):
                            rows = P if kt < FULL else TAIL
                            dve.wait_ge(gpT_psum, nth * (FULL + 1) + kt + 1)
                            if kt >= 2:
                                dve.wait_ge(go_done, nth * (FULL + 1) + kt - 1)
                            v.tensor_copy(pT[0:rows, kt % 2, :], ps[0][0:rows, (kt % 2) * BANK:(kt % 2) * BANK + P]).then_inc(gpT_ready, 1)
                        dve.wait_ge(go_done, (nth + 1) * (FULL + 1))
                        lstep(v.reciprocal(gen[:, 5:6], gen[:, 2:3]), 7)
                        lstep(v.tensor_scalar(xn_flat[:, bass.ds(t * C + h * D, D)], po[0][:, 0:D],
                                              gen[:, 5:6], None, ALU.mult), 8)
                v.tensor_copy(gen[:, 6:7], gen[:, 0:1]).then_inc(gfin_ready, 1)
                dve.wait_ge(gfin_psum, 1)
                glink(v.tensor_scalar(vmean[:, 0, :], po[1][:, 0:C], 1.0 / NK, None, ALU.mult))
                glink(v.tensor_scalar(gen[:, 7:8], po[0][:, 0:1], 0.5, None, ALU.is_gt))
                glink(v.tensor_scalar(vmean[:, 1, :].bitcast(U32), ones[:, :], gen[:, 7:8], None, ALU.mult))
                for t in range(QT):
                    last = v.copy_predicated(att_tok[:, t, :], vmean[:, 1, :].bitcast(U32), vmean[:, 0, :])
                last.then_inc(attention_done, NHALF)
                take_first_attT()
                residual(0, po[0][:, :], glink)

            tlink = chain(tail_step)
            layernorm(2, halves[0], tlink)
            residual(1, bank(5), tlink)
            layernorm(3, halves[1], tlink)
            dve.wait_ge(xnT_ready, 2 * NHALF)
            v.tensor_tensor(msum[:, 2:3], msum[:, 0:1], msum[:, 1:2], ALU.add).then_inc(msum_ready, 1)
            dve.wait_ge(logit_psum, 1)
            dve.wait_ge(ffn_in, 16 * FFN_LOADS)
            tlink(v.scalar_tensor_tensor(gate[0:1, 0, :], po[0][0:1, 0:E], 1.0 / NQ, bg[:, :], ALU.mult, ALU.add))
            tlink(v.tensor_reduce(gate[0:1, 4, 0:1], gate[0:1, 0, :], AX.X, ALU.max))
            v.tensor_scalar(gate[0:1, 1, :], gate[0:1, 0, :], gate[0:1, 4, 0:1], None, ALU.subtract).then_inc(msum_ready, 1)
            dve.wait_ge(exp_gate, 1)
            tlink(v.reciprocal(gate[0:1, 4, 1:2], gate[0:1, 3, 0:1]))
            tlink(v.tensor_scalar(gate[0:1, 5, :], gate[0:1, 2, :], gate[0:1, 4, 1:2], None, ALU.mult))
            tlink(v.max(gate[0:1, 6, :], gate[0:1, 5, :]))
            v.max_index(topi[:, :], gate[0:1, 6, :], gate[0:1, 5, :]).then_inc(topk_ready, 1)
            tlink(v.tensor_tensor(gate[0:1, 4, 2:3], gate[0:1, 6, 0:1], gate[0:1, 6, 1:2], ALU.add))
            tlink(v.reciprocal(gate[0:1, 4, 3:4], gate[0:1, 4, 2:3]))
            v.tensor_scalar(mix[0:1, 1:3], gate[0:1, 6, 0:TOPK], gate[0:1, 4, 3:4], gate[0:1, 7, 0:1], ALU.mult, ALU.mult).then_inc(mix_ready, 1)
            dve.wait_ge(topk_ready, 1)
            for e in range(TOPK):
                i = dve.value_load(topi[0:1, e:e + 1], min_val=0, max_val=E - 1)
                last = v.tensor_copy(b1s[:, e, :], b1T[:, bass.ds(i * CB, CB)])
            last.then_inc(b1s_ready, 1)
            dve.wait_ge(mixb_psum, 1)
            v.tensor_copy(mixb[:, 1:3], bank(MIX_BANK)[:, 0:TOPK]).then_inc(mixb_taken, 1)
            dve.wait_ge(mixb_taken, 1)
            dve.wait_ge(experts_in, 16 * 3 * TOPK)
            for e in range(TOPK):
                v.tensor_scalar(w2s[:, e, :, :], w2s[:, e, :, :], mixb[:, 1 + e:2 + e], None, ALU.mult).then_inc(w2_scaled, 1)
            dve.wait_ge(mix_ready, 1)
            tlink(v.tensor_scalar(bsum[0:1, 1, :], b2rows[0:1, 0, :], mix[0:1, 0:1], None, ALU.mult))
            tlink(v.scalar_tensor_tensor(bsum[0:1, 2, :], b2rows[0:1, 1, :], mix[0:1, 1:2], bsum[0:1, 1, :], ALU.mult, ALU.add))
            v.scalar_tensor_tensor(bsum[0:1, 0, :], b2rows[0:1, 2, :], mix[0:1, 2:3], bsum[0:1, 2, :], ALU.mult, ALU.add).then_inc(bsum_ready, 1)
            for n in range(NHALF):
                dve.wait_ge(ffn_psum, n + 1)
                v.tensor_tensor(xn[:, n * QT // 2:(n + 1) * QT // 2, :],
                                po[n][:, :].rearrange("p (t c) -> p t c", c=C),
                                xres[:, n * QT // 2:(n + 1) * QT // 2, :], ALU.add).then_inc(res_ready, 1)

        @block.tensor
        def _(pe):
            mm, tr = nc.tensor.matmul, nc.tensor.transpose
            pe.wait_ge(const_ready, 3)

            def ctx_transpose(c):
                if c >= 3:
                    pe.wait_ge(ctxT_ready, c - 2)
                dst, at = bank(c % 3, CK), 0
                for t in range(4 * c, min(4 * c + 4, FULL)):
                    pe.wait_ge(ctx_in[sum(t >= b for b in CTX_AT[1:])], 16)
                    last = tr(dst[:, at:at + P], ctx_sb[:, t, :], ident[:, :])
                    at += P
                if c == KCH - 1:
                    pe.wait_ge(tail_in, 16)
                    last = tr(dst[:, at:at + TAIL], ctx_tail[:, :], ident[0:TAIL, 0:TAIL])
                last.then_inc(ctxT_psum, 1)

            def project_k(c):
                a, b = c * BANK, min((c + 1) * BANK, NK)
                pe.wait_ge(ctxT_ready, c + 1)
                if c >= 3:
                    pe.wait_ge(k_ready, c - 2)
                mm(bank(3 + c % 3, P, b - a), wk_sb[:, :], ctxT[0:CK, a:b], start=True, stop=True).then_inc(k_psum, 1)

            def project_v(nth):
                c = V_ORDER[nth]
                if nth >= 2:
                    pe.wait_ge(v_done, nth - 1)
                for t in range(4 * c, min(4 * c + 4, FULL + 1)):
                    if t == FULL:
                        pe.wait_ge(tailT_ready, 1)
                    lhsT = ctxT[:, t * P:(t + 1) * P] if t < FULL else tailT[:, :]
                    last = mm(po[nth % 2][:, (t % 4) * P:(t % 4 + 1) * P], lhsT, wv_sb[:, :], start=True, stop=True)
                last.then_inc(v_psum, 1)

            for c in range(3):
                ctx_transpose(c)
            pe.wait_ge(wk_in, 16)
            project_k(0)
            ctx_transpose(3)
            project_k(1)
            for n in range(NHALF):
                for t in range(n * QT // 2, (n + 1) * QT // 2):
                    pe.wait_ge(xn_ready, t + 1)
                    last = tr(po[n][:, (t % 4) * P:(t % 4 + 1) * P], xn[:, t, :], ident[:, :])
                last.then_inc(xnT_psum, 1)
            ctx_transpose(4)
            project_k(2)
            pe.wait_ge(wts_in, 48)
            for n in range(NHALF):
                pe.wait_ge(xnT_ready, n + 1)
                mm(po[n][:, :], wq_sb[:, :], xnT[:, n * BANK:(n + 1) * BANK], start=True, stop=True).then_inc(q_psum, 1)
            for c in range(3, KCH):
                if c + 2 < KCH:
                    ctx_transpose(c + 2)
                project_k(c)
            pe.wait_ge(ffn_in, 16 * FFN_LOADS)
            pe.wait_ge(k_ready, KCH - 2)
            rows = bank(BO_BANK)
            mm(rows[:, 0:C], ones[0:1, :], bsum[0:1, 0, :], start=True, stop=True)
            mm(rows[:, ALPHA_COL:ALPHA_COL + 1], ones[0:1, :], mix[0:1, 3:4], start=True, stop=True)
            tr(rows[:, C:C + (E + 1) * CB], b1rows[:, :], ident[0:(E + 1) * CB, 0:(E + 1) * CB]).then_inc(rows_psum, 1)
            pe.wait_ge(wv_in, 32)
            pe.wait_ge(pads_ready, 2)
            pe.wait_ge(q_abs_ready, NHALF)
            for c in range(VCH):
                if c == VCH - FLAG_AHEAD:
                    pe.wait_ge(rows_taken, 1)
                    pe.wait_ge(flag_ready, 1)
                    safe = pe.value_load(flag[0:1, 0:1], min_val=0, max_val=1)
                project_v(c)
                if c == BOUND_AT:
                    pe.wait_ge(bounds_ready, 2)
                    for n in range(NHALF):
                        last = mm(ps[0][0:2 * H, n * BANK:(n + 1) * BANK], bounds[:, :], q_abs[:, n * BANK:(n + 1) * BANK], start=True, stop=True)
                    last.then_inc(bound_psum, 1)
                if c == BOUND_AT + 4:
                    pe.wait_ge(gcol_ready, 1)
                    mm(ps[0][0:1, 0:2 * H], gcol[:, 1:2], ident[0:2 * H, 0:2 * H], start=True, stop=True)
                    mm(ps[0][0:1, BANK:BANK + 1], kcol[:, 4:5], ones[:, 0:1], start=True, stop=True).then_inc(grow_psum, 1)
            def att_transpose(n, dst):
                pe.wait_ge(attention_done, n + 1)
                for i, t in enumerate(range(n * QT // 2, (n + 1) * QT // 2)):
                    last = tr(dst[:, i * P:(i + 1) * P], att_tok[:, t, :], ident[:, :])
                last.then_inc(attT_psum, 1)

            def project_out(n, dst):
                pe.wait_ge(attT_ready, n + 1)
                for i, t in enumerate(range(n * QT // 2, (n + 1) * QT // 2)):
                    last = mm(dst[:, i * P:(i + 1) * P], attT[:, t * P:(t + 1) * P], wo_sb[:, :], start=True, stop=True)
                last.then_inc(y_psum, 1)

            with pe.If(safe != 0):
                def last_to_tokens(n):
                    pe.wait_ge(o_taken, NHALF * (NG - 1) + n + 1)
                    for i, t in enumerate(range(n * QT // 2, (n + 1) * QT // 2)):
                        last = tr(po[0][:, i * P:(i + 1) * P], oraw[:, (NG - 1) % 2, t * P:(t + 1) * P], ident[:, :])
                    last.then_inc(tok_psum, 1)

                def free_slot(slot):
                    if slot < NSB:
                        return
                    kind, nth = taker(slot - NSB)
                    if kind == "norm":
                        pe.wait_ge(tok_taken, nth + 1)
                    else:
                        pe.wait_ge(exp_ready, nth + 1)

                def score_tile(t):
                    g, i = divmod(t, TL_G)
                    slot = slot_of_tile(t)
                    free_slot(slot)
                    for m in range(CPT):
                        kt, half, j, _ = CHUNKS[g][CPT * i + m]
                        if kt < FULL and kt % SEG_T == 0 and half == 0 and j == 0:
                            pe.wait_ge(kst_in[kt // SEG_T], 16 * 2 * PARTS * (g + 1))
                        if CPT * i + m == 0:
                            pe.wait_ge(qst_in[g % 2], 16 * PARTS * PARTS * (g // 2 + 1))
                        queries = slice(half * BANK, (half + 1) * BANK)
                        dst = ps[slot % NSB][:, m * BANK:(m + 1) * BANK]
                        for jj in ([j] if kt < FULL else range(GH)):
                            keys, q = kst[jj // 2][0:ROWS, jj % 2, :], qst[:, g % 2, jj, queries]
                            if kt < FULL:
                                last = mm(dst, keys[:, kt * P:(kt + 1) * P], q, start=True, stop=True)
                            else:
                                last = mm(dst[QUAD * jj:QUAD * (jj + 1), :], keys[:, kt * P:kt * P + QUAD], q,
                                          start=True, stop=True, skip_group_check=True)
                    last.then_inc(scores_ready, 1)

                def values_step(g, n):
                    kt, half = STEPS[g][n]
                    first = all(h != half for _, h in STEPS[g][:n])
                    final = all(h != half for _, h in STEPS[g][n + 1:])
                    if half == 0 and kt < FULL and kt % SEG_T == 0:
                        pe.wait_ge(vst_ready, g * NSEG + kt // SEG_T + 1)
                    if g >= 1 and first:
                        pe.wait_ge(o_taken, (g - 1) * NHALF + half + 1)
                    for c, (_, _, j, step) in enumerate(CHUNKS[g]):
                        if step != n:
                            continue
                        t, m = divmod(c, CPT)
                        src = probs[:, (g * TL_G + t) % NPR, m * BANK:(m + 1) * BANK]
                        if kt < FULL:
                            last = mm(po[half][QUAD * j:QUAD * (j + 1), :], vst[:, kt, QUAD * j:QUAD * (j + 1)], src,
                                      start=first, stop=final, skip_group_check=True)
                        else:
                            last = mm(po[half][:, :], vtail[:, :], src, start=first, stop=final, skip_group_check=True)
                    last.then_inc(pv_done, 1)

                def group_to_tokens(g):
                    slot = slot_of_norm(g)
                    free_slot(slot)
                    pe.wait_ge(o_taken, NHALF * (g + 1))
                    for t in range(QT):
                        last = tr(ps[slot % NSB][:, t * P:(t + 1) * P], oraw[:, g % 2, t * P:(t + 1) * P], ident[:, :])
                    last.then_inc(tok_psum, 1)

                for t in range(NSB):
                    score_tile(t)
                for t in range(NG * TL_G):
                    g, i = divmod(t, TL_G)
                    if t + NSB < NG * TL_G:
                        if t + NSB > TL_G and (t + NSB - NORM_AT) % TL_G == 0:
                            group_to_tokens((t + NSB) // TL_G - 1)
                        score_tile(t + NSB)
                    pe.wait_ge(exp_ready, t + 1)
                    for n in range(QD_G):
                        if max(c for c, chunk in enumerate(CHUNKS[g]) if chunk[3] == n) // CPT == i:
                            values_step(g, n)
                    if g == NG - 1 and i == EARLY_AT:
                        last_to_tokens(0)
                    if g == NG - 1 and i == EARLY_AT + EARLY_GAP:
                        att_transpose(0, po[0])
                    if g == NG - 1 and i == EARLY_AT + 2 * EARLY_GAP:
                        project_out(0, po[0])
                pe.wait_ge(y_taken, 1)
                last_to_tokens(1)
            with pe.Else():
                with pe.Fori(0, H) as h:
                    with pe.Fori(0, QT) as t:
                        nth = h * QT + t
                        pe.wait_ge(gq_ready, nth + 1)
                        for c in range(KCH):
                            a, b = c * BANK, min((c + 1) * BANK, NK)
                            if c >= 2:
                                pe.wait_ge(gs_copied, nth * KCH + c - 1)
                            mm(ps[1][:, (c % 2) * BANK:(c % 2) * BANK + b - a], qm[:, :], kT[:, a:b], start=True, stop=True).then_inc(gs_psum, 1)
                        pe.wait_ge(gexp_ready, nth + 1)
                        for kt in range(FULL + 1):
                            rows = P if kt < FULL else TAIL
                            if kt >= 2:
                                pe.wait_ge(gpT_ready, nth * (FULL + 1) + kt - 1)
                            tr(ps[0][0:rows, (kt % 2) * BANK:(kt % 2) * BANK + P], srow[:, kt * P:kt * P + rows], ident[:, :]).then_inc(gpT_psum, 1)
                            pe.wait_ge(gpT_ready, nth * (FULL + 1) + kt + 1)
                            mm(po[0][:, 0:D], pT[0:rows, kt % 2, :], vall[0:rows, kt, bass.ds(h * D, D)],
                               start=(kt == 0), stop=(kt == FULL)).then_inc(go_done, 1)
                pe.wait_ge(gfin_ready, 1)
                mm(po[0][:, 0:1], ones[:, :], gen[:, 6:7], start=True, stop=True)
                for kt in range(FULL + 1):
                    rows = P if kt < FULL else TAIL
                    last = mm(po[1][:, 0:C], ones[0:rows, :], vall[0:rows, kt, :], start=(kt == 0), stop=(kt == FULL))
                last.then_inc(gfin_psum, 1)
                att_transpose(0, po[0])
                project_out(0, po[0])
            att_transpose(1, bank(4))
            project_out(1, bank(5))

            def xn_transpose(n):
                for i, t in enumerate(range(n * QT // 2, (n + 1) * QT // 2)):
                    pe.wait_ge(xn_ready, QT + t + 1)
                    last = tr(po[n][:, i * P:(i + 1) * P], xn[:, t, :], ident[:, :])
                last.then_inc(xnT_psum, 1)

            def first_layer(e, steps):
                for r in steps:
                    n = e * CB * NHALF + r
                    half, cb = divmod(r, CB)
                    if n >= 6:
                        pe.wait_ge(hid_ready, n - 5)
                    w = w1m_sb[:, cb * P:(cb + 1) * P] if e == 0 else w1s[:, e - 1, cb * P:(cb + 1) * P]
                    mm(bank(n % 6), w,
                       xnT[:, half * BANK:(half + 1) * BANK], start=True, stop=True).then_inc(hid_psum, 1)

            def second_layer(e, half):
                pe.wait_ge(hid_ready, e * CB * NHALF + CB * (half + 1))
                pe.wait_ge(w2_scaled, e + 1)
                if e == TOPK:
                    pe.wait_ge(bsum_ready, 1)
                w2 = w2m_sb if e == 0 else w2s[:, e - 1, :, :]
                for t in range(half * QT // 2, (half + 1) * QT // 2):
                    dst = po[t // 4][:, (t % 4) * P:(t % 4 + 1) * P]
                    for cb in range(CB):
                        last = mm(dst, hid[e % 2][:, cb, t * P:(t + 1) * P], w2[:, cb, :],
                                  start=(e == 0 and cb == 0 and t % 4 == 0), stop=False, skip_group_check=True)
                    if e == TOPK:
                        last = mm(dst, ones[0:1, :], bsum[0:1, 0, :], start=False, stop=True, skip_group_check=True)
                        if t % 4 == 3:
                            last.then_inc(ffn_psum, 1)
                if e < TOPK and half == 1:
                    last.then_inc(ffn2_done, 1)

            xn_transpose(0)
            pe.wait_ge(xnT_ready, NHALF + 1)
            first_layer(0, range(CB))
            xn_transpose(1)
            pe.wait_ge(msum_ready, 1)
            mm(po[0][0:1, 0:E], msum[:, 2:3], wg[:, :], start=True, stop=True).then_inc(logit_psum, 1)
            first_layer(0, range(CB, CB * NHALF))
            pe.wait_ge(msum_ready, 2)
            second_layer(0, 0)
            pe.wait_ge(mix_ready, 1)
            mm(bank(MIX_BANK)[:, 0:TOPK], ones[0:1, :], mix[0:1, 1:3], start=True, stop=True).then_inc(mixb_psum, 1)
            second_layer(0, 1)
            pe.wait_ge(experts_in, 16 * 3 * TOPK)
            pe.wait_ge(mixb_taken, 1)
            for e in range(1, TOPK + 1):
                first_layer(e, range(CB * NHALF))
            for e in range(1, TOPK + 1):
                for half in range(NHALF):
                    second_layer(e, half)


_OUT = ((1, NQ, C), "float32")


def kernel(x, ctx_768, L0_xattn_Wq, L0_xattn_bq, L0_xattn_Wk, L0_xattn_bk, L0_xattn_Wv, L0_xattn_bv, L0_xattn_Wo,
           L0_xattn_bo, L0_ffn_alpha, L0_ffn_w_gate, L0_ffn_b_gate, L0_ffn_W1m, L0_ffn_b1m, L0_ffn_W2m, L0_ffn_b2m,
           L0_ffn_W1e, L0_ffn_b1e, L0_ffn_W2e, L0_ffn_b2e):
    import numpy as np
    import concourse.bacc as bacc
    from concourse.bass_utils import run_bass_kernel_spmd

    shaped = {
        "x": x, "ctx": ctx_768, "wq": L0_xattn_Wq, "bq": np.reshape(L0_xattn_bq, (C, 1)), "wk": L0_xattn_Wk,
        "bk": np.reshape(L0_xattn_bk, (C, 1)), "wv": L0_xattn_Wv, "bv": np.reshape(L0_xattn_bv, (1, C)),
        "wo": L0_xattn_Wo, "bo": np.reshape(L0_xattn_bo, (1, C)), "alpha": np.reshape(L0_ffn_alpha, (1, 1)),
        "w_gate": L0_ffn_w_gate, "b_gate": np.reshape(L0_ffn_b_gate, (1, E)), "w1m": L0_ffn_W1m,
        "b1m": np.reshape(L0_ffn_b1m, (1, HID)), "w2m": L0_ffn_W2m, "b2m": np.reshape(L0_ffn_b2m, (1, C)),
        "w1e": L0_ffn_W1e, "b1e": L0_ffn_b1e, "w2e": L0_ffn_W2e, "b2e": L0_ffn_b2e,
    }
    nc = bacc.Bacc("TRN2", target_bir_lowering=False, num_devices=1)
    arrays, aps = {}, {}
    for name, value in shaped.items():
        a = np.ascontiguousarray(value)
        arrays[f"in_{name}"] = a
        aps[name] = nc.dram_tensor(f"in_{name}", a.shape, mybir.dt.from_np(a.dtype), kind="ExternalInput").ap()
    shape, dtype = _OUT
    out = nc.dram_tensor("result", shape, mybir.dt.from_np(np.dtype(dtype)), kind="ExternalOutput").ap()
    build(nc, **aps, out=out)
    r = run_bass_kernel_spmd(nc, [arrays], core_ids=[0])
    return r.results[0]["result"]
```
